# Optimizing a Trainium2 kernel written in Bass

```python
import numpy as np
import jax
import jax.numpy as jnp

def _softmax(x, axis=-1):
    return jax.nn.softmax(x, axis=axis)

def _gelu(x):
    return jax.nn.gelu(x, approximate=True)

def _silu(x):
    return jax.nn.silu(x)

def _sigmoid(x):
    return jax.nn.sigmoid(x)

def _layernorm(x, axis=-1, eps=1e-05):
    m = jnp.mean(x, axis=axis, keepdims=True)
    v = jnp.var(x, axis=axis, keepdims=True)
    return (x - m) / jnp.sqrt(v + eps)

def _scatter_add(tgt, idx, src, axis=0):
    return tgt.at[idx].add(src)

def _segment_sum(src, seg, n):
    return jax.ops.segment_sum(src, seg, n)
kernel_name = 'mk_decoder_preln_d1_seqx_r4_39f440'

def setup_inputs(seed: int=0):
    np.random.seed(seed)
    _w = jnp.asarray

    def _rec_inputs():
        import jax
        import jax.numpy as jnp
        _rk = jax.random.key(seed)
        x = 7.22e-05 + 1 * jax.random.normal(jax.random.fold_in(_rk, 1), (16, 128, 256), jnp.float32)
        _lenS = 128 - jax.random.randint(jax.random.fold_in(_rk, 7), (16,), 0, max(1, 128 // 4) + 1, jnp.int32)
        _lenS2 = 128 - jax.random.randint(jax.random.fold_in(_rk, 8), (16,), 0, max(1, 128 // 4) + 1, jnp.int32)
        _ctx_1024P = jax.random.normal(jax.random.fold_in(_rk, 11), (16, 16, 256), jnp.float32)
        _ctx_1024c = jax.random.dirichlet(jax.random.fold_in(_rk, 511), 0.3 * jnp.ones((16,), jnp.float32), (16, 128))
        _ctx_1024t = jnp.einsum('bsk,bkd->bsd', _ctx_1024c, _ctx_1024P)
        _ctx_1024t = _ctx_1024t * jax.lax.rsqrt(jnp.mean(jnp.square(_ctx_1024t)) + 1e-12) * 0.953939
        ctx_1024 = 4.13588e-05 + 0.999923 * (_ctx_1024t + 0.3 * jax.random.normal(jax.random.fold_in(_rk, 611), (16, 128, 256), jnp.float32))
        return (x, ctx_1024)
    x, ctx_1024 = _rec_inputs()

    def _L0_attn_setup():
        import jax, jax.numpy as jnp
        import numpy as np
        DIM = 256
        HEADS = 16
        HEAD_DIM = DIM // HEADS // 2
        DEPTH = 12
        LAMBDA_INIT = 0.8 - 0.6 * float(np.exp(-0.3 * DEPTH))
        EPS = 1e-05
        B, N = (2, 512)
        key = jax.random.key(seed)
        ks = jax.random.split(key, 9)
        s = 0.02
        return {'x': jax.random.normal(ks[0], (B, N, DIM), jnp.float32), 'W_qkv': jax.random.normal(ks[1], (DIM, 3 * DIM), jnp.float32) * s, 'W_proj': jax.random.normal(ks[2], (DIM, DIM), jnp.float32) * s, 'b_proj': jnp.zeros((DIM,), jnp.float32), 'lambda_q1': jax.random.normal(ks[3], (HEAD_DIM,), jnp.float32) * 0.1, 'lambda_k1': jax.random.normal(ks[4], (HEAD_DIM,), jnp.float32) * 0.1, 'lambda_q2': jax.random.normal(ks[5], (HEAD_DIM,), jnp.float32) * 0.1, 'lambda_k2': jax.random.normal(ks[6], (HEAD_DIM,), jnp.float32) * 0.1, 'subln_w': jnp.ones((2 * HEAD_DIM,), jnp.float32)}
    _L0_attn_all = _L0_attn_setup()
    _L0_attn_in = {k: v for k, v in _L0_attn_all.items() if k in ('W_qkv', 'W_proj', 'b_proj', 'lambda_q1', 'lambda_k1', 'lambda_q2', 'lambda_k2', 'subln_w')}
    del _L0_attn_all

    def _L0_xattn_setup():
        import jax, jax.numpy as jnp
        import numpy as np
        TEMPERATURE = 8.0
        D = 256
        key = jax.random.key(seed)
        ks = jax.random.split(key, 11)
        B, S = (4, 512)
        scale = 1.0 / np.sqrt(D)
        return {'q': jax.random.normal(ks[0], (B, S, D), dtype=jnp.float32), 'k': jax.random.normal(ks[1], (B, S, D), dtype=jnp.float32), 'v': jax.random.normal(ks[2], (B, S, D), dtype=jnp.float32), 'Wq': jax.random.normal(ks[3], (D, D), dtype=jnp.float32) * scale, 'bq': jax.random.normal(ks[4], (D,), dtype=jnp.float32) * 0.02, 'Wk': jax.random.normal(ks[5], (D, D), dtype=jnp.float32) * scale, 'bk': jax.random.normal(ks[6], (D,), dtype=jnp.float32) * 0.02, 'Wv': jax.random.normal(ks[7], (D, D), dtype=jnp.float32) * scale, 'bv': jax.random.normal(ks[8], (D,), dtype=jnp.float32) * 0.02, 'Wf': jax.random.normal(ks[9], (D, D), dtype=jnp.float32) * scale, 'bf': jax.random.normal(ks[10], (D,), dtype=jnp.float32) * 0.02}
    _L0_xattn_all = _L0_xattn_setup()
    _L0_xattn_in = {k: v for k, v in _L0_xattn_all.items() if k in ('Wq', 'bq', 'Wk', 'bk', 'Wv', 'bv', 'Wf', 'bf')}
    del _L0_xattn_all

    def _L0_ffn_setup():
        import jax, jax.numpy as jnp
        import numpy as np
        B, S, D = (4, 1024, 256)
        H = 1024
        RH = 256
        E = 16
        K = 2
        NS = 1

        def _swiglu(x, w1, w2, w3):
            return jax.nn.silu(x @ w1) * (x @ w2) @ w3
        key = jax.random.key(seed)
        ks = jax.random.split(key, 9)
        s = 0.02
        return {'x': jax.random.normal(ks[0], (B, S, D), dtype=jnp.float32), 'router_w': jax.random.normal(ks[1], (D, E), dtype=jnp.float32) * s, 'expert_bias': jnp.zeros((E,), dtype=jnp.float32), 'shared_w1': jax.random.normal(ks[2], (NS, D, H), dtype=jnp.float32) * s, 'shared_w2': jax.random.normal(ks[3], (NS, D, H), dtype=jnp.float32) * s, 'shared_w3': jax.random.normal(ks[4], (NS, H, D), dtype=jnp.float32) * s, 'routed_w1': jax.random.normal(ks[5], (E, D, RH), dtype=jnp.float32) * s, 'routed_w2': jax.random.normal(ks[6], (E, D, RH), dtype=jnp.float32) * s, 'routed_w3': jax.random.normal(ks[7], (E, RH, D), dtype=jnp.float32) * s}
    _L0_ffn_all = _L0_ffn_setup()
    _L0_ffn_in = {k: v for k, v in _L0_ffn_all.items() if k in ('router_w', 'expert_bias', 'shared_w1', 'shared_w2', 'shared_w3', 'routed_w1', 'routed_w2', 'routed_w3')}
    del _L0_ffn_all
    return {'x': x, 'ctx_1024': ctx_1024, 'L0_attn_W_qkv': _L0_attn_in['W_qkv'], 'L0_attn_W_proj': _L0_attn_in['W_proj'], 'L0_attn_b_proj': _L0_attn_in['b_proj'], 'L0_attn_lambda_q1': _L0_attn_in['lambda_q1'], 'L0_attn_lambda_k1': _L0_attn_in['lambda_k1'], 'L0_attn_lambda_q2': _L0_attn_in['lambda_q2'], 'L0_attn_lambda_k2': _L0_attn_in['lambda_k2'], 'L0_attn_subln_w': _L0_attn_in['subln_w'], 'L0_xattn_Wq': _L0_xattn_in['Wq'], 'L0_xattn_bq': _L0_xattn_in['bq'], 'L0_xattn_Wk': _L0_xattn_in['Wk'], 'L0_xattn_bk': _L0_xattn_in['bk'], 'L0_xattn_Wv': _L0_xattn_in['Wv'], 'L0_xattn_bv': _L0_xattn_in['bv'], 'L0_xattn_Wf': _L0_xattn_in['Wf'], 'L0_xattn_bf': _L0_xattn_in['bf'], 'L0_ffn_router_w': _L0_ffn_in['router_w'], 'L0_ffn_expert_bias': _L0_ffn_in['expert_bias'], 'L0_ffn_shared_w1': _L0_ffn_in['shared_w1'], 'L0_ffn_shared_w2': _L0_ffn_in['shared_w2'], 'L0_ffn_shared_w3': _L0_ffn_in['shared_w3'], 'L0_ffn_routed_w1': _L0_ffn_in['routed_w1'], 'L0_ffn_routed_w2': _L0_ffn_in['routed_w2'], 'L0_ffn_routed_w3': _L0_ffn_in['routed_w3']}

def reference(x, ctx_1024, L0_attn_W_qkv, L0_attn_W_proj, L0_attn_b_proj, L0_attn_lambda_q1, L0_attn_lambda_k1, L0_attn_lambda_q2, L0_attn_lambda_k2, L0_attn_subln_w, L0_xattn_Wq, L0_xattn_bq, L0_xattn_Wk, L0_xattn_bk, L0_xattn_Wv, L0_xattn_bv, L0_xattn_Wf, L0_xattn_bf, L0_ffn_router_w, L0_ffn_expert_bias, L0_ffn_shared_w1, L0_ffn_shared_w2, L0_ffn_shared_w3, L0_ffn_routed_w1, L0_ffn_routed_w2, L0_ffn_routed_w3):
    import jax
    import jax.numpy as jnp

    def _L0_attn_ref(x, W_qkv, W_proj, b_proj, lambda_q1, lambda_k1, lambda_q2, lambda_k2, subln_w):
        import jax, jax.numpy as jnp
        import numpy as np
        DIM = 256
        HEADS = 16
        HEAD_DIM = DIM // HEADS // 2
        DEPTH = 12
        LAMBDA_INIT = 0.8 - 0.6 * float(np.exp(-0.3 * DEPTH))
        EPS = 1e-05
        B, N = (2, 512)
        Bm, Nm, C = x.shape
        H, hd = (HEADS, HEAD_DIM)
        scale = hd ** (-0.5)
        qkv = (x @ W_qkv).reshape(Bm, Nm, 3, H, 2 * hd)
        q, k, v = (qkv[:, :, 0], qkv[:, :, 1], qkv[:, :, 2])
        q = q.reshape(Bm, Nm, 2 * H, hd).transpose(0, 2, 1, 3)
        k = k.reshape(Bm, Nm, 2 * H, hd).transpose(0, 2, 1, 3)
        v = v.transpose(0, 2, 1, 3)
        q1, q2 = (q[:, :H], q[:, H:])
        k1, k2 = (k[:, :H], k[:, H:])

        def sdpa(qh, kh):
            scores = jnp.einsum('bhqd,bhkd->bhqk', qh, kh) * scale
            a = jax.nn.softmax(scores, axis=-1)
            return jnp.einsum('bhqk,bhkd->bhqd', a, v)
        attn1 = sdpa(q1, k1)
        attn2 = sdpa(q2, k2)
        lam1 = jnp.exp(jnp.sum(lambda_q1 * lambda_k1))
        lam2 = jnp.exp(jnp.sum(lambda_q2 * lambda_k2))
        lam = lam1 - lam2 + LAMBDA_INIT
        o = attn1 - lam * attn2
        o = o * jax.lax.rsqrt(jnp.mean(o * o, axis=-1, keepdims=True) + EPS)
        o = o * subln_w
        o = o * (1.0 - LAMBDA_INIT)
        o = o.transpose(0, 2, 1, 3).reshape(Bm, Nm, C)
        return o @ W_proj + b_proj

    def _L0_xattn_ref(q, k, v, Wq, bq, Wk, bk, Wv, bv, Wf, bf):
        import jax, jax.numpy as jnp
        import numpy as np
        TEMPERATURE = 8.0
        D = 256
        residual = v
        qp = jnp.einsum('bsd,ed->bse', q, Wq) + bq
        kp = jnp.einsum('bsd,ed->bse', k, Wk) + bk
        vp = jnp.einsum('bsd,ed->bse', v, Wv) + bv
        attn = jnp.einsum('bqd,bkd->bqk', qp / TEMPERATURE, kp)
        attn = jax.nn.softmax(attn, axis=-1)
        context = jnp.einsum('bqk,bkd->bqd', attn, vp)
        context = jax.nn.gelu(jnp.einsum('bsd,ed->bse', context, Wf) + bf, approximate=False)
        return context + residual

    def _L0_ffn_ref(x, router_w, expert_bias, shared_w1, shared_w2, shared_w3, routed_w1, routed_w2, routed_w3):
        import jax, jax.numpy as jnp
        import numpy as np
        B, S, D = (4, 1024, 256)
        H = 1024
        RH = 256
        E = 16
        K = 2
        NS = 1

        def _swiglu(x, w1, w2, w3):
            return jax.nn.silu(x @ w1) * (x @ w2) @ w3
        shared_out = jnp.sum(jax.vmap(lambda w1, w2, w3: _swiglu(x, w1, w2, w3))(shared_w1, shared_w2, shared_w3), axis=0)
        scores = jax.nn.sigmoid(x @ router_w)
        sel_scores = scores + expert_bias
        _, top_idx = jax.lax.top_k(sel_scores, K)
        top_scores = jnp.take_along_axis(scores, top_idx, axis=-1)
        gates = jnp.sum(jax.nn.one_hot(top_idx, E, dtype=scores.dtype) * top_scores[..., None], axis=-2)
        xf = x.reshape(-1, D)
        gf = gates.reshape(-1, E).T

        def body(acc, ws):
            w1, w2, w3, g = ws
            return (acc + _swiglu(xf, w1, w2, w3) * g[:, None], None)
        routed_out, _ = jax.lax.scan(body, jnp.zeros_like(xf), (routed_w1, routed_w2, routed_w3, gf))
        return shared_out + routed_out.reshape(x.shape)
    x = x + _L0_attn_ref(_layernorm(x, axis=-1), L0_attn_W_qkv, L0_attn_W_proj, L0_attn_b_proj, L0_attn_lambda_q1, L0_attn_lambda_k1, L0_attn_lambda_q2, L0_attn_lambda_k2, L0_attn_subln_w)
    x = x + _L0_xattn_ref(_layernorm(x, axis=-1), ctx_1024, ctx_1024, L0_xattn_Wq, L0_xattn_bq, L0_xattn_Wk, L0_xattn_bk, L0_xattn_Wv, L0_xattn_bv, L0_xattn_Wf, L0_xattn_bf)
    x = x + _L0_ffn_ref(_layernorm(x, axis=-1), L0_ffn_router_w, L0_ffn_expert_bias, L0_ffn_shared_w1, L0_ffn_shared_w2, L0_ffn_shared_w3, L0_ffn_routed_w1, L0_ffn_routed_w2, L0_ffn_routed_w3)
    return x

_drawn_inputs = setup_inputs


def setup_inputs(seed=0):
    import zlib

    import numpy as np

    out = dict(_drawn_inputs(seed))
    spreads = {'L0_attn_b_proj': (0.0, 0.1),
     'L0_attn_subln_w': (1.0, 0.6),
     'L0_ffn_expert_bias': (0.0, 0.757)}
    factors = {'L0_attn_lambda_q1': 64.0,
     'L0_attn_lambda_k1': 64.0,
     'L0_attn_lambda_q2': 8.0,
     'L0_attn_lambda_k2': 8.0,
     'L0_xattn_bq': 8.0,
     'L0_xattn_bk': 64.0,
     'L0_xattn_bv': 6.996,
     'L0_xattn_bf': 6.474,
     'L0_ffn_router_w': 8.0,
     'L0_ffn_routed_w1': 6.282,
     'L0_ffn_routed_w2': 6.201,
     'L0_ffn_routed_w3': 6.192,
     'L0_ffn_shared_w1': 8.0,
     'L0_ffn_shared_w2': 8.0,
     'L0_ffn_shared_w3': 8.0}
    for name, (base, spread) in spreads.items():
        noise = np.random.default_rng([zlib.crc32(name.encode()), seed]).standard_normal(out[name].shape)
        drawn = base * np.exp(spread * noise) if base else spread * noise
        out[name] = jnp.asarray(drawn.astype(out[name].dtype))
    for name, factor in factors.items():
        out[name] = (out[name] * factor).astype(out[name].dtype)
    return out
```

```python
from contextlib import ExitStack

import numpy as np

import concourse.bass as bass
from concourse import mybir

ALU = mybir.AluOpType
ACT = mybir.ActivationFunctionType
F32 = mybir.dt.float32
BF16 = mybir.dt.bfloat16
I32 = mybir.dt.int32
AX_X = mybir.AxisListType.X
ds = bass.ds

P = 128
NB, D = 16, 256
T = NB * P
KT = D // P
H, HD = 16, 8
NMAP = 2 * H
VD = 2 * HD
VP = 32
LAMBDA_INIT = 0.8 - 0.6 * float(np.exp(-0.3 * 12))
EPS = 1e-5
FLT_MAX = float(np.finfo(np.float32).max)
SQ_MAX = (FLT_MAX / VD) ** 0.5 * (1 - 2.0 ** -20)
SUM_MAX = FLT_MAX / VD ** 2
TEMPERATURE = 8.0
NE, RH, SH = 16, 256, 1024
NS = SH // RH
NX = NS + NE
CB = 4
NC = NB // CB
CT = CB * P
PAIRS = [(0, 0), (0, 1), (1, 0), (1, 1), (0, 2), (2, 0)]
KQ = len(PAIRS) * HD
KM = KQ + 3
START = 4096


class Line:

    def __init__(self, eng, sem, step=1, hold=None):
        self.eng, self.sem, self.step, self.hold = eng, sem, step, hold
        self.base, self.k = 0, 0

    def mark(self, ins):
        ins.then_inc(self.sem, self.step)
        self.k += self.step
        return (self, self.base, self.k)

    def last(self):
        return (self, self.base, self.k)

    def wait(self, *tokens):
        for line, base, k in tokens:
            self.eng.wait_ge(line.sem, base + k)
            if self.hold is not None and not isinstance(base, int):
                self.eng.sem_inc(self.hold, 1)

    def settle(self):
        self.wait(self.last())


class Loop:

    def __init__(self, nc, n, lines, name):
        self.nc, self.n, self.lines, self.name, self.per = nc, n, lines, name, PER[name]

    def __enter__(self):
        self.cm = self.nc.Fori(0, self.n)
        self.i = self.cm.__enter__()
        self.outer = [(l.base, l.k) for l in self.lines]
        for l, per in zip(self.lines, self.per):
            l.base, l.k = self.i * per + (l.base + l.k), 0
        return self.i

    def __exit__(self, *exc):
        if exc[0] is None:
            got = [l.k for l in self.lines]
            assert got == self.per, f"{self.name} marks per iteration: {got}"
        r = self.cm.__exit__(*exc)
        for l, per, (base, k) in zip(self.lines, self.per, self.outer):
            l.base, l.k = base, k + per * self.n
        return r


def decoder_layer(nc, x, ctx_1024, W_qkv, W_proj, b_proj, lq1, lk1, lq2, lk2, subln_w,
                  Wq, bq, Wk, bk, Wv, bv, Wf, bf, router_w, expert_bias,
                  sw1, sw2, sw3, rw1, rw2, rw3, out, qk_parts, upto=99, dbg=None):
    es = ExitStack()
    with es:
        def sb(name, shape, dt=F32, stack=es):
            return stack.enter_context(nc.sbuf_tensor(name, shape, dt))

        ps = es.enter_context(nc.psum_tensor("ps", [P, 8, 512], F32))

        def sem(name):
            return es.enter_context(nc.semaphore(name))

        V = Line(nc.vector, sem("done_vector"), hold=sem("hold_vector"))
        A = Line(nc.scalar, sem("done_scalar"))
        M = Line(nc.tensor, sem("done_tensor"))
        G = Line(nc.gpsimd, sem("done_gpsimd"), hold=sem("hold_gpsimd"))
        hold_sync = sem("hold_sync")
        Lw = Line(nc.sync, sem("loads_once"), 16, hold_sync)
        Lc = Line(nc.sync, sem("loads_of_chunk"), 16, hold_sync)
        Lm = Line(nc.sync, sem("loads_of_maxima"), 16, hold_sync)
        lines = [V, A, M, G, Lw, Lc, Lm]
        compute = [V, A, M, G]

        def join():
            marks = [l.last() for l in lines]
            for e in compute:
                e.wait(*marks)
            Lw.wait(*marks[:4])

        X = sb("X", [P, NB, D])
        ident = sb("ident", [P, P])
        identb = sb("identb", [P, P], BF16)
        st = sb("st", [P, CB, 6])
        mv = sb("mv", [P, CB, 2])
        rstd = sb("rstd", [P, CB])
        xn = sb("xn", [P, CB, D])
        xT = sb("xT", [P, KT, CT])
        va = sb("va", [P, 64])
        y = sb("y", [P, 64])
        t1 = sb("t1", [P, 64])
        bp_b = sb("bp_b", [P, D])
        bv_b = sb("bv_b", [P, D])
        bf_b = sb("bf_b", [P, D])
        bq_c = sb("bq_c", [P, KT])
        bk_c = sb("bk_c", [P, KT])
        sub_c = sb("sub_c", [P, 1])
        lam = sb("lam", [P, 4, HD])
        lw = sb("lw", [P, 8])
        neg_lam = sb("neg_lam", [P, 1])
        Wp = sb("Wp", [P, H // 4, D])
        WT = {n: sb("WT" + n, [P, KT, D]) for n in ("q", "k", "v", "f")}
        Ob = sb("Ob", [P, NB, 4, 4, VD])

        def load(dst, src):
            return Lw.mark(nc.sync.dma_start(dst, src))

        def row(v, n):
            return v.rearrange("(o n) -> o n", o=1).to_broadcast([P, n])

        def inv_sqrt(v, n):
            yi = y[:, 0:n].bitcast(I32)
            V.mark(nc.vector.tensor_scalar(yi, v.bitcast(I32), 1, None, ALU.logical_shift_right))
            V.settle()
            V.mark(nc.vector.tensor_scalar(yi, yi, -1.0, float(0x5F3759DF), ALU.mult, ALU.add))
            V.settle()
            for _ in range(3):
                V.mark(nc.vector.tensor_tensor(t1[:, 0:n], y[:, 0:n], y[:, 0:n], ALU.mult))
                V.settle()
                V.mark(nc.vector.scalar_tensor_tensor(t1[:, 0:n], t1[:, 0:n], -0.5, v, ALU.mult, ALU.mult))
                V.settle()
                tok = V.mark(nc.vector.scalar_tensor_tensor(y[:, 0:n], t1[:, 0:n], 1.5, y[:, 0:n],
                                                            ALU.add, ALU.mult))
                V.settle()
            return tok

        def layernorm_T(c):
            for j in range(CB):
                V.mark(nc.vector.bn_stats(st[:, j, :], X[:, ds(c * CB + j, 1), :].rearrange("p o d -> p (o d)")))
            V.settle()
            for j in range(CB):
                V.mark(nc.vector.bn_aggr(mv[:, j, :], st[:, j, :]))
            V.settle()
            V.mark(nc.vector.tensor_scalar(va[:, 0:CB], mv[:, :, 1], EPS, None, ALU.add))
            V.settle()
            inv_sqrt(va[:, 0:CB], CB)
            copied = []
            for j in range(CB):
                n = V.mark(nc.vector.tensor_scalar(xn[:, j, :], X[:, ds(c * CB + j, 1), :].rearrange("p o d -> p (o d)"),
                                                   mv[:, j, 0:1], y[:, j:j + 1], ALU.subtract, ALU.mult))
                M.wait(n)
                if j >= 2:
                    M.wait(copied[j - 2])
                for k in range(KT):
                    r = nc.tensor.transpose(ps[:, j % 2, k * P:(k + 1) * P], xn[:, j, k * P:(k + 1) * P], ident[:, :])
                turned = M.mark(r)
                A.wait(turned)
                copied.append(A.mark(nc.scalar.activation(
                    xT[:, :, j * P:(j + 1) * P], ps[:, j % 2, 0:D].rearrange("p (k t) -> p k t", k=KT), ACT.Copy)))
            return copied

        for l in compute:
            l.eng.sem_inc(l.sem, START)
            l.k = START
        with nc.allow_non_contiguous_dma(reason="short vectors, once"):
            load(bq_c[:, :], bq.rearrange("(t p) -> p t", p=P))
            load(bk_c[:, :], bk.rearrange("(t p) -> p t", p=P))
        xv = x.rearrange("b p d -> p b d")
        for c in range(NC):
            load(X[:, c * CB:(c + 1) * CB, :], xv[:, c * CB:(c + 1) * CB, :])
        for dst, src, n in ((bp_b, b_proj, D), (bv_b, bv, D), (bf_b, bf, D)):
            load(dst[:, :], row(src, n))
        for i, v in enumerate((lq1, lk1, lq2, lk2)):
            load(lam[:, i, :], row(v, HD))
        zeroed = V.mark(nc.vector.memset(Wp[:, :, :], 0.0))
        zeroed = V.mark(nc.vector.memset(sub_c[:, :], 0.0))
        Lw.wait(V.last())
        for j in range(4):
            load(Wp[32 * j:32 * j + VD, :, :], W_proj.rearrange("(a j d) n -> j d a n", j=4, d=VD)[j])
            load(sub_c[32 * j:32 * j + VD, :], subln_w.rearrange("(d o) -> d o", o=1))
        G.mark(nc.gpsimd.memset(ident[:, :], 0.0))
        G.settle()
        G.mark(nc.gpsimd.affine_select(out=ident[:, :], in_=ident[:, :], compare_op=ALU.not_equal, fill=1.0,
                                       base=0, pattern=[[-1, P]], channel_multiplier=1))
        V.wait(G.last())
        V.mark(nc.vector.tensor_copy(identb[:, :], ident[:, :]))

        p1 = ExitStack()
        Wqkv = sb("Wqkv", [P, KT, 3 * D], F32, p1)
        Vt = sb("Vt", [P, NB, H, VD], F32, p1)
        p0 = ExitStack()
        Wraw = sb("Wraw", [P, 4, KT, D], F32, p0)
        load(Wqkv[:, :, :], W_qkv.rearrange("(k p) n -> p k n", p=P))
        for i, w in enumerate((Wq, Wk, Wv, Wf)):
            load(Wraw[:, i, :, :], w.rearrange("(e p) d -> p e d", p=P))
        join()
        for i, n in enumerate(("q", "k", "v", "f")):
            for e in range(KT):
                for k in range(KT):
                    r = nc.tensor.transpose(ps[:, i, k * D + e * P:k * D + (e + 1) * P],
                                            Wraw[:, i, e, k * P:(k + 1) * P], ident[:, :])
            A.wait(M.mark(r))
            A.mark(nc.scalar.activation(WT[n][:, :, :], ps[:, i, :].rearrange("p (k e) -> p k e", k=KT), ACT.Copy))
        for i in range(2):
            V.mark(nc.vector.tensor_tensor(lam[:, 2 * i, :], lam[:, 2 * i, :], lam[:, 2 * i + 1, :], ALU.mult))
        V.settle()
        for i in range(2):
            V.mark(nc.vector.tensor_reduce(lw[:, i:i + 1], lam[:, 2 * i, :], AX_X, ALU.add))
        A.wait(V.last())
        A.mark(nc.scalar.activation(lw[:, 2:4], lw[:, 0:2], ACT.Exp))
        V.wait(A.last())
        V.mark(nc.vector.tensor_tensor(lw[:, 4:5], lw[:, 3:4], lw[:, 2:3], ALU.subtract))
        V.settle()
        V.mark(nc.vector.tensor_scalar(neg_lam[:, :], lw[:, 4:5], -LAMBDA_INIT, None, ALU.add))
        V.mark(nc.vector.tensor_scalar(Wp[:, :, :], Wp[:, :, :], sub_c[:, 0:1], 1.0 - LAMBDA_INIT,
                                       ALU.mult, ALU.mult))
        join()
        p0.close()

        with ExitStack() as s1:
            part = sb("part", [P, 3, 4, CT], BF16, s1)
            rest = sb("rest", [P, 2, CT], F32, s1)
            with Loop(nc, NC, lines, "qkv") as c:
                join()
                ready = layernorm_T(c)
                M.wait(ready[-1])
                first, third = {}, {}
                for f in range(4):
                    bank = 2 + f
                    for k in range(KT):
                        r = nc.tensor.matmul(ps[:, bank, :], Wqkv[:, k, f * P:(f + 1) * P], xT[:, k, :],
                                             start=(k == 0), stop=(k == KT - 1))
                    made = M.mark(r)
                    A.wait(made)
                    first[f] = A.mark(nc.scalar.activation(part[:, 0, f, :], ps[:, bank, :], ACT.Copy))
                    V.wait(first[f])
                    if f >= 2:
                        V.wait(third[f - 2])
                    V.mark(nc.vector.tensor_tensor(rest[:, f % 2, :], ps[:, bank, :], part[:, 0, f, :], ALU.subtract))
                    V.settle()
                    second = V.mark(nc.vector.tensor_copy(part[:, 1, f, :], rest[:, f % 2, :]))
                    G.wait(second)
                    third[f] = G.mark(nc.gpsimd.tensor_tensor(part[:, 2, f, :], rest[:, f % 2, :], part[:, 1, f, :],
                                                              ALU.subtract))
                vcopied = []
                for j in range(CB):
                    if j >= 2:
                        M.wait(vcopied[j - 2])
                    for k in range(KT):
                        r = nc.tensor.matmul(ps[:, 6 + j % 2, 0:D], xT[:, k, j * P:(j + 1) * P],
                                             Wqkv[:, k, 2 * D:3 * D], start=(k == 0), stop=(k == KT - 1))
                    A.wait(M.mark(r))
                    vcopied.append(A.mark(nc.scalar.activation(
                        Vt[:, ds(c * CB + j, 1), :, :].rearrange("p o h d -> p (o h d)"), ps[:, 6 + j % 2, 0:D], ACT.Copy)))
                for q in range(3):
                    Lc.wait((first[3], second, third[3])[q])
                    Lc.mark(nc.sync.dma_start(qk_parts[q, :, :, ds(c * CT, CT)].rearrange("f p t -> p f t"),
                                              part[:, q, :, :]))
            join()

        with ExitStack() as s2:
            packs = [[sb(f"pack_{n}{u}", [64, NMAP, 2 * P], BF16, s2) for u in range(2)] for n in "qk"]
            Qp, Kp = packs
            Vs = sb("Vs", [P, 2, H, VP], F32, s2)
            nmax = sb("nmax", [P, 2, NMAP], F32, s2)
            mrest = sb("mrest", [P, 2, NMAP], F32, s2)
            mpart = sb("mpart", [P, 2, 3 * NMAP], BF16, s2)
            mT = sb("mT", [3 * NMAP, 2, P], BF16, s2)
            prob = sb("prob", [P, 4, 512], F32, s2)
            OT = sb("OT", [P, 2, 1024], F32, s2)
            rden = sb("rden", [P, 2, 4, 2, 4], F32, s2)
            o2 = sb("o2", [P, 4, 4, VD], F32, s2)
            o1 = sb("o1", [P, 4, 4, VD], F32, s2)
            for u in range(2):
                V.mark(nc.vector.memset(Kp[u][32:64, :, :], 1.0))
            G.mark(nc.gpsimd.memset(Vs[:, :, :, :], 0.0))
            G.settle()
            G.mark(nc.gpsimd.memset(Vs[:, :, :, VD:VD + 1], 1.0))
            with Loop(nc, NC, lines, "attn") as c:
                join()
                landed = []
                for u in range(2):
                    for dst, f0, which in ((Qp, 0, 0), (Kp, 2, 1)):
                        for r, pr in enumerate(PAIRS):
                            src = qk_parts[pr[which], f0:f0 + 2, :, ds(c * CT + u * 2 * P, 2 * P)]
                            for f in range(2):
                                Lc.mark(nc.sync.dma_start(dst[u][r * HD:(r + 1) * HD, f * H:(f + 1) * H, :],
                                                          src[f].rearrange("(h d) t -> d h t", d=HD)))
                    landed.append(Lc.last())
                landed = [landed[1]] * 2
                maxed, mput, exped, pv_done, otr, vsd, comb = {}, {}, {}, {}, {}, {}, {}

                def scores(u, g):
                    lo = (u % 2) * P
                    M.wait(landed[u // 2])
                    n = u * 8 + g
                    if n >= 2:
                        M.wait(maxed[n - 2])
                    for m in range(4):
                        j = 4 * g + m
                        r = nc.tensor.matmul(ps[:, g % 2, m * P:(m + 1) * P], Qp[u // 2][0:KQ, j, lo:lo + P],
                                             Kp[u // 2][0:KQ, j, lo:lo + P], start=True, stop=True)
                    V.wait(M.mark(r))
                    maxed[n] = V.mark(nc.vector.tensor_reduce(
                        nmax[:, u % 2, 4 * g:4 * g + 4], ps[:, g % 2, :].rearrange("p (m t) -> p m t", m=4),
                        AX_X, ALU.max, negate=True))

                def put_max(u):
                    b, lo = u % 2, (u % 2) * P
                    if u >= 2:
                        V.wait(mput[u - 2][0])
                    V.settle()
                    V.mark(nc.vector.tensor_copy(mpart[:, b, 0:NMAP], nmax[:, b, :]))
                    V.settle()
                    V.mark(nc.vector.tensor_tensor(mrest[:, b, :], nmax[:, b, :], mpart[:, b, 0:NMAP], ALU.subtract))
                    V.settle()
                    V.mark(nc.vector.tensor_copy(mpart[:, b, NMAP:2 * NMAP], mrest[:, b, :]))
                    V.settle()
                    V.mark(nc.vector.tensor_tensor(mpart[:, b, 2 * NMAP:], mrest[:, b, :], mpart[:, b, NMAP:2 * NMAP],
                                                   ALU.subtract))
                    M.wait(V.last())
                    if u >= 1:
                        M.wait(mput[u - 1][1])
                    turned = M.mark(nc.tensor.transpose(ps[0:3 * NMAP, 7, 0:P // 2].bitcast(BF16), mpart[:, b, :],
                                                        identb[:, :]))
                    A.wait(turned)
                    if u >= 2:
                        A.wait(mput[u - 2][2])
                    copied = A.mark(nc.scalar.activation(mT[:, b, :], ps[0:3 * NMAP, 7, 0:P // 2].bitcast(BF16), ACT.Copy))
                    Lm.wait(copied)
                    for q in range(3):
                        put = Lm.mark(nc.sync.dma_start(Qp[u // 2][KQ + q:KQ + q + 1, :, lo:lo + P],
                                                        mT[q * NMAP:(q + 1) * NMAP, b, :]))
                    mput[u] = (turned, copied, put)

                def exps(u, g):
                    lo, n = (u % 2) * P, u * 8 + g
                    bank = 2 + n % 3
                    M.wait(mput[u][2])
                    if n >= 3:
                        M.wait(exped[n - 3])
                    for hh in range(2):
                        for m in range(2):
                            j = m * H + 2 * g + hh
                            r = nc.tensor.matmul(ps[:, bank, (2 * hh + m) * P:(2 * hh + m + 1) * P],
                                                 Kp[u // 2][0:KM, j, lo:lo + P], Qp[u // 2][0:KM, j, lo:lo + P],
                                                 start=True, stop=True)
                    A.wait(M.mark(r))
                    if n >= 4:
                        A.wait(pv_done[n - 4])
                    exped[n] = A.mark(nc.scalar.activation(prob[:, n % 4, :], ps[:, bank, :], ACT.Exp, scale=HD ** -0.5))

                def values(u):
                    if u >= 2:
                        G.wait(pv_done[(u - 2) * 8 + 7])
                    vsd[u] = G.mark(nc.gpsimd.tensor_copy(
                        Vs[:, u % 2, :, 0:VD], Vt[:, ds(c * CB + u, 1), :, :].rearrange("p o h d -> p (o h) d")))

                def pv(u, g):
                    n, bank = u * 8 + g, 5 + g // 4
                    M.wait(exped[n], vsd[u])
                    if u >= 1 and g % 4 == 0:
                        M.wait(otr[(u - 1, g // 4)])
                    for hh in range(2):
                        h = 2 * g + hh
                        q, col = 32 * (h % 4), (h // 4 % 2) * 2 * P
                        r = nc.tensor.matmul(ps[q:q + VP, bank, col:col + 2 * P], Vs[:, u % 2, h, :],
                                             prob[:, n % 4, hh * 2 * P:(hh + 1) * 2 * P], start=True, stop=True,
                                             tile_position=(0, q))
                    pv_done[n] = M.mark(r)

                def turn(u, half):
                    V.wait(pv_done[u * 8 + half * 4 + 3])
                    if u >= 2:
                        V.wait(comb[u - 2])
                    otr[(u, half)] = V.mark(nc.vector.transpose(OT[:, u % 2, half * 512:(half + 1) * 512],
                                                                ps[:, 5 + half, :]))

                def combine(u):
                    o = OT[:, u % 2, :].rearrange("p (a m k d) -> p a m k d", a=4, m=2, k=4)
                    if u >= 2:
                        V.wait(comb[u - 2])
                    V.settle()
                    rd = rden[:, u % 2, :, :, :]
                    for m in range(2):
                        V.mark(nc.vector.reciprocal(rd[:, :, m, :], o[:, :, m, :, VD]))
                    V.settle()
                    V.mark(nc.vector.tensor_scalar(rd[:, :, 1, :], rd[:, :, 1, :], neg_lam[:, 0:1], None, ALU.mult))
                    G.wait(V.last())

                    def by(m):
                        return rd[:, :, m, :].unsqueeze(3).to_broadcast([P, 4, 4, VD])
                    G.mark(nc.gpsimd.tensor_tensor(o1[:, :, :, :], o[:, :, 0, :, 0:VD], by(0), ALU.mult))
                    G.mark(nc.gpsimd.tensor_tensor(o2[:, :, :, :], o[:, :, 1, :, 0:VD], by(1), ALU.mult))
                    G.settle()
                    comb[u] = G.mark(nc.gpsimd.tensor_tensor(
                        Ob[:, ds(c * CB + u, 1), :, :, :].rearrange("p o a k d -> p (o a k d)"),
                        o1[:, :, :, :].rearrange("p a k d -> p (a k d)"),
                        o2[:, :, :, :].rearrange("p a k d -> p (a k d)"), ALU.add))
                    G.settle()

                LEAD = 4
                values(0)
                for g in range(8):
                    scores(0, g)
                put_max(0)
                for u in range(CB):
                    if u + 1 < CB:
                        values(u + 1)
                        for g in range(LEAD):
                            scores(u + 1, g)
                    for g in range(8):
                        exps(u, g)
                        if u + 1 < CB and g + LEAD < 8:
                            scores(u + 1, g + LEAD)
                        if g == 8 - LEAD and u + 1 < CB:
                            put_max(u + 1)
                        if g >= 1:
                            pv(u, g - 1)
                        if g == 4 + 1:
                            turn(u, 0)
                    pv(u, 7)
                    turn(u, 1)
                    combine(u)
            join()
        p1.close()
        if upto == 2:
            fin = Lw.mark(nc.sync.dma_start(dbg, Ob[:, :, :, :, :].rearrange("p b a k d -> p (b a k d)")))
            nc.sync.wait_ge(Lw.sem, Lw.k)
            return

        with ExitStack() as s3:
            ONp = sb("ONp", [P, CB, 16, VP], F32, s3)
            sq = sb("sq", [P, CB * 16, VD], F32, s3)
            fits = sb("fits", [P, CB * 16], F32, s3)
            oT = sb("oT", [P, CB, 4, P], F32, s3)
            Cx = sb("Cx", [P, CB, D], F32, s3)
            cT = sb("cT", [P, KT, CT], F32, s3)
            qT = sb("qT", [P, KT, CT], F32, s3)
            kT = sb("kT", [P, KT, CT], F32, s3)
            vp = sb("vp", [P, CB, D], F32, s3)
            nm = sb("nm", [P, CB], F32, s3)
            den = sb("den", [P, CB], F32, s3)
            pr_ = sb("pr_", [P, CB, P], F32, s3)
            pT = sb("pT", [P, CB, P], F32, s3)
            coT = sb("coT", [P, CB, KT, P], F32, s3)
            fo = sb("fo", [P, CB, D], F32, s3)
            V.mark(nc.vector.memset(ONp[:, :, :, :], 0.0))
            cv = ctx_1024.rearrange("b p d -> p b d")
            with Loop(nc, NC, lines, "cross") as c:
                join()
                Lc.mark(nc.sync.dma_start(Cx[:, :, :], cv[:, ds(c * CB, CB), :]))
                o = Ob[:, ds(c * CB, CB), :, :, :].rearrange("p b a k d -> p (b a k) d")
                V.mark(nc.vector.tensor_scalar(sq[:, :, :], o, 1.0 / VD, SQ_MAX, ALU.mult, ALU.min))
                V.settle()
                V.mark(nc.vector.tensor_scalar(sq[:, :, :], sq[:, :, :], -SQ_MAX, None, ALU.max))
                A.wait(V.last())
                A.mark(nc.scalar.activation(sq[:, :, :], sq[:, :, :], ACT.Square))
                V.wait(A.last())
                V.mark(nc.vector.tensor_reduce(va[:, :], sq[:, :, :], AX_X, ALU.add))
                V.settle()
                V.mark(nc.vector.tensor_scalar(fits[:, :], va[:, :], SUM_MAX, None, ALU.is_le))
                V.mark(nc.vector.tensor_scalar(va[:, :], va[:, :], SUM_MAX, float(VD), ALU.min, ALU.mult))
                V.settle()
                V.mark(nc.vector.tensor_scalar(va[:, :], va[:, :], EPS, None, ALU.add))
                V.settle()
                inv_sqrt(va[:, :], 64)
                V.mark(nc.vector.tensor_tensor(y[:, :], y[:, :], fits[:, :], ALU.mult))
                V.settle()
                V.mark(nc.vector.tensor_tensor(ONp[:, :, :, 0:VD].rearrange("p b a d -> p (b a) d"), o,
                                               y[:, :].unsqueeze(2).to_broadcast([P, 64, VD]), ALU.mult))
                V.settle()
                turned = V.mark(nc.vector.transpose(oT[:, :, :, :].rearrange("p b a t -> p (b a t)"),
                                                    ONp[:, :, :, :].rearrange("p b a d -> p (b a d)")))
                M.wait(turned)
                for j in range(CB):
                    for a in range(4):
                        r = nc.tensor.matmul(ps[:, 2 + j, 0:D], oT[:, j, a, :], Wp[:, a, :],
                                             start=(a == 0), stop=(a == 3))
                    V.wait(M.mark(r))
                    xj = X[:, ds(c * CB + j, 1), :].rearrange("p o d -> p (o d)")
                    V.mark(nc.vector.tensor_tensor(xj, ps[:, 2 + j, 0:D], xj, ALU.add))
                V.settle()
                for j in range(CB):
                    xj = X[:, ds(c * CB + j, 1), :].rearrange("p o d -> p (o d)")
                    V.mark(nc.vector.tensor_tensor(xj, xj, bp_b[:, :], ALU.add))
                V.settle()
                M.wait(Lc.last())
                G.wait(Lc.last())
                cc = []
                for j in range(CB):
                    if j >= 2:
                        M.wait(cc[j - 2])
                    for k in range(KT):
                        r = nc.tensor.transpose(ps[:, 6 + j % 2, k * P:(k + 1) * P], Cx[:, j, k * P:(k + 1) * P],
                                                ident[:, :])
                    A.wait(M.mark(r))
                    cc.append(A.mark(nc.scalar.activation(
                        cT[:, :, j * P:(j + 1) * P], ps[:, 6 + j % 2, 0:D].rearrange("p (k t) -> p k t", k=KT),
                        ACT.Copy)))
                xr = layernorm_T(c)
                M.wait(cc[-1], xr[-1], V.last())
                for i, (dst, w, b, src) in enumerate(((kT, "k", bk_c, cT), (qT, "q", bq_c, xT))):
                    for e in range(KT):
                        for k in range(KT):
                            r = nc.tensor.matmul(ps[:, 2 + 2 * i + e, :], WT[w][:, k, e * P:(e + 1) * P], src[:, k, :],
                                                 start=(k == 0), stop=(k == KT - 1))
                        A.wait(M.mark(r))
                        A.mark(nc.scalar.activation(dst[:, e, :], ps[:, 2 + 2 * i + e, :], ACT.Identity, bias=b[:, e:e + 1]))
                qk_ready = A.last()
                vd = []
                for j in range(CB):
                    if j >= 2:
                        M.wait(vd[j - 2])
                    for k in range(KT):
                        r = nc.tensor.matmul(ps[:, 6 + j % 2, 0:D], cT[:, k, j * P:(j + 1) * P], WT["v"][:, k, :],
                                             start=(k == 0), stop=(k == KT - 1))
                    V.wait(M.mark(r))
                    vd.append(V.mark(nc.vector.tensor_tensor(vp[:, j, :], ps[:, 6 + j % 2, 0:D], bv_b[:, :], ALU.add)))
                M.wait(qk_ready)
                for j in range(CB):
                    for k in range(KT):
                        r = nc.tensor.matmul(ps[:, j, 0:P], qT[:, k, j * P:(j + 1) * P], kT[:, k, j * P:(j + 1) * P],
                                             start=(k == 0), stop=(k == KT - 1))
                    V.wait(M.mark(r))
                    V.mark(nc.vector.tensor_reduce(nm[:, j:j + 1], ps[:, j, 0:P], AX_X, ALU.max, negate=True))
                V.settle()
                V.mark(nc.vector.tensor_scalar(nm[:, :], nm[:, :], 1.0 / TEMPERATURE, None, ALU.mult))
                A.wait(V.last())
                for j in range(CB):
                    A.mark(nc.scalar.activation(pr_[:, j, :], ps[:, j, 0:P], ACT.Exp, scale=1.0 / TEMPERATURE,
                                                bias=nm[:, j:j + 1], accum_out=den[:, j:j + 1]))
                V.wait(A.last())
                V.mark(nc.vector.reciprocal(den[:, :], den[:, :]))
                V.settle()
                for j in range(CB):
                    V.mark(nc.vector.tensor_scalar(pr_[:, j, :], pr_[:, j, :], den[:, j:j + 1], None, ALU.mult))
                    M.wait(V.last())
                    A.wait(M.mark(nc.tensor.transpose(ps[:, 4, j * P:(j + 1) * P], pr_[:, j, :], ident[:, :])))
                tp = A.mark(nc.scalar.activation(pT[:, :, :].rearrange("p b t -> p (b t)"), ps[:, 4, :], ACT.Copy))
                M.wait(tp)
                for j in range(CB):
                    for e in range(KT):
                        r = nc.tensor.matmul(ps[:, j, e * P:(e + 1) * P], vp[:, j, e * P:(e + 1) * P], pT[:, j, :],
                                             start=True, stop=True)
                    A.wait(M.mark(r))
                    done = A.mark(nc.scalar.activation(coT[:, j, :, :].rearrange("p k t -> p (k t)"), ps[:, j, 0:D],
                                                       ACT.Copy))
                    M.wait(done)
                    for k in range(KT):
                        r = nc.tensor.matmul(ps[:, 4 + j, 0:D], coT[:, j, k, :], WT["f"][:, k, :],
                                             start=(k == 0), stop=(k == KT - 1))
                    V.wait(M.mark(r))
                    V.mark(nc.vector.tensor_tensor(fo[:, j, :], ps[:, 4 + j, 0:D], bf_b[:, :], ALU.add))
                A.wait(V.last())
                A.mark(nc.scalar.activation(fo[:, :, :], fo[:, :, :], ACT.Gelu))
                G.wait(A.last())
                G.mark(nc.gpsimd.tensor_tensor(fo[:, :, :], fo[:, :, :], Cx[:, :, :], ALU.add))
                G.settle()
                xc = X[:, ds(c * CB, CB), :]
                G.mark(nc.gpsimd.tensor_tensor(xc, xc, fo[:, :, :], ALU.add))
            join()
        if upto == 3:
            fin = Lw.mark(nc.sync.dma_start(dbg, X[:, :, :].rearrange("p b d -> p (b d)")))
            nc.sync.wait_ge(Lw.sem, Lw.k)
            return

        with ExitStack() as s4:
            W12 = sb("W12", [P, NX, KT, 2 * RH], F32, s4)
            W3 = sb("W3", [P, NX, KT, D], F32, s4)
            Wr = sb("Wr", [P, KT, NE], F32, s4)
            eb = sb("eb", [P, NE], F32, s4)
            back = sb("back", [P, NE], F32, s4)
            sc = sb("sc", [P, CB, NE], F32, s4)
            sel = sb("sel", [P, CB, NE], F32, s4)
            eq = sb("eq", [P, CB, NE], F32, s4)
            top = sb("top", [P, CB], F32, s4)
            chosen = sb("chosen", [P, CB, NE], F32, s4)
            gate = sb("gate", [P, CB, NX], F32, s4)
            sa = sb("sa", [P, CB, RH], F32, s4)
            hT = sb("hT", [P, CB, KT, P], F32, s4)
            load(Wr[:, :, :], router_w.rearrange("(k p) e -> p k e", p=P))
            load(eb[:, :], row(expert_bias, NE))
            for s in range(NS):
                for i, w in enumerate((sw1, sw2)):
                    load(W12[:, s, :, i * RH:(i + 1) * RH],
                         w[0].rearrange("(k p) f -> p k f", p=P)[:, :, s * RH:(s + 1) * RH])
            load(W3[:, 0:NS, :, :], sw3[0].rearrange("(s k p) d -> p s k d", p=P, k=KT))
            for e in range(NE):
                for i, w in enumerate((rw1, rw2)):
                    load(W12[:, NS + e, :, i * RH:(i + 1) * RH], w[e].rearrange("(k p) f -> p k f", p=P))
                load(W3[:, NS + e, :, :], rw3[e].rearrange("(k p) d -> p k d", p=P))
            G.mark(nc.gpsimd.iota(back[:, :], pattern=[[-1, NE]], base=NE, channel_multiplier=0,
                                  allow_small_or_imprecise_dtypes=True))
            V.mark(nc.vector.memset(gate[:, :, 0:NS], 1.0))
            with Loop(nc, NC, lines, "experts") as c:
                join()
                xr = layernorm_T(c)
                M.wait(xr[-1])
                for j in range(CB):
                    for k in range(KT):
                        r = nc.tensor.matmul(ps[:, 2, j * NE:(j + 1) * NE], xT[:, k, j * P:(j + 1) * P], Wr[:, k, :],
                                             start=(k == 0), stop=(k == KT - 1))
                A.wait(M.mark(r))
                A.mark(nc.scalar.activation(sc[:, :, :].rearrange("p j e -> p (j e)"), ps[:, 2, 0:CB * NE], ACT.Sigmoid))
                V.wait(A.last())

                def vec(ins):
                    V.mark(ins)
                    V.settle()

                def wide(v):
                    return v[:, :].unsqueeze(1).to_broadcast([P, CB, NE])

                def per_token(v):
                    return v[:, :].unsqueeze(2).to_broadcast([P, CB, NE])

                def flat(v):
                    return v[:, :, :].rearrange("p j e -> p (j e)")
                vec(nc.vector.tensor_tensor(sel[:, :, :], sc[:, :, :], wide(eb), ALU.add))
                for pick in range(2):
                    vec(nc.vector.tensor_reduce(top[:, :], sel[:, :, :], AX_X, ALU.max))
                    vec(nc.vector.tensor_tensor(eq[:, :, :], sel[:, :, :], per_token(top), ALU.is_equal))
                    vec(nc.vector.tensor_tensor(eq[:, :, :], eq[:, :, :], wide(back), ALU.mult))
                    vec(nc.vector.tensor_reduce(top[:, :], eq[:, :, :], AX_X, ALU.max))
                    if pick == 0:
                        vec(nc.vector.tensor_tensor(chosen[:, :, :], eq[:, :, :], per_token(top), ALU.is_equal))
                        vec(nc.vector.scalar_tensor_tensor(flat(sel), flat(chosen), -3.0e38, flat(sel), ALU.mult, ALU.add))
                    else:
                        vec(nc.vector.tensor_tensor(eq[:, :, :], eq[:, :, :], per_token(top), ALU.is_equal))
                        vec(nc.vector.tensor_tensor(chosen[:, :, :], chosen[:, :, :], eq[:, :, :], ALU.add))
                vec(nc.vector.tensor_tensor(gate[:, :, NS:], sc[:, :, :], chosen[:, :, :], ALU.mult))
                with Loop(nc, NX, lines, "expert") as e:
                    join()
                    up, act, had, tr, cp, down, added = {}, {}, {}, {}, {}, {}, {}
                    for j in range(CB):
                        for k in range(KT):
                            r = nc.tensor.matmul(ps[:, j, :], xT[:, k, j * P:(j + 1) * P],
                                                 W12[:, ds(e, 1), k, :].rearrange("p o f -> p (o f)"),
                                                 start=(k == 0), stop=(k == KT - 1))
                        up[j] = M.mark(r)
                        A.wait(up[j])
                        act[j] = A.mark(nc.scalar.activation(sa[:, j, :], ps[:, j, 0:RH], ACT.Silu))
                        V.wait(act[j])
                        had[j] = V.mark(nc.vector.tensor_tensor(sa[:, j, :], sa[:, j, :], ps[:, j, RH:2 * RH], ALU.mult))

                    def flip(j):
                        M.wait(had[j])
                        if j >= 2:
                            M.wait(cp[j - 2])
                        for k in range(KT):
                            r = nc.tensor.transpose(ps[:, 4 + j % 2, k * P:(k + 1) * P], sa[:, j, k * P:(k + 1) * P],
                                                    ident[:, :])
                        A.wait(M.mark(r))
                        cp[j] = A.mark(nc.scalar.activation(hT[:, j, :, :].rearrange("p k t -> p (k t)"),
                                                            ps[:, 4 + j % 2, 0:D], ACT.Copy))

                    def lower(j):
                        M.wait(cp[j])
                        if j >= 2:
                            M.wait(added[j - 2])
                        for k in range(KT):
                            r = nc.tensor.matmul(ps[:, 6 + j % 2, 0:D], hT[:, j, k, :],
                                                 W3[:, ds(e, 1), k, :].rearrange("p o f -> p (o f)"),
                                                 start=(k == 0), stop=(k == KT - 1))
                        V.wait(M.mark(r))
                        xj = X[:, ds(c * CB + j, 1), :].rearrange("p o d -> p (o d)")
                        added[j] = V.mark(nc.vector.scalar_tensor_tensor(
                            xj, ps[:, 6 + j % 2, 0:D], gate[:, j, ds(e, 1)], xj, ALU.mult, ALU.add))
                    flip(0)
                    flip(1)
                    for j in range(CB):
                        lower(j)
                        if j + 2 < CB:
                            flip(j + 2)
                Lc.wait(V.last())
                Lc.mark(nc.sync.dma_start(out.rearrange("b p d -> p b d")[:, ds(c * CB, CB), :],
                                          X[:, ds(c * CB, CB), :]))
            nc.sync.wait_ge(Lc.sem, Lc.base + Lc.k)
            join()


PER = {
    "qkv": [32, 12, 12, 4, 0, 48, 0],
    "attn": [68, 36, 100, 16, 0, 768, 192],
    "cross": [70, 23, 36, 2, 0, 16, 0],
    "experts": [198, 165, 245, 0, 0, 16, 0],
    "expert": [8, 8, 12, 0, 0, 0, 0],
}

_INS = ['x', 'ctx_1024', 'L0_attn_W_qkv', 'L0_attn_W_proj', 'L0_attn_b_proj', 'L0_attn_lambda_q1',
        'L0_attn_lambda_k1', 'L0_attn_lambda_q2', 'L0_attn_lambda_k2', 'L0_attn_subln_w', 'L0_xattn_Wq',
        'L0_xattn_bq', 'L0_xattn_Wk', 'L0_xattn_bk', 'L0_xattn_Wv', 'L0_xattn_bv', 'L0_xattn_Wf', 'L0_xattn_bf',
        'L0_ffn_router_w', 'L0_ffn_expert_bias', 'L0_ffn_shared_w1', 'L0_ffn_shared_w2', 'L0_ffn_shared_w3',
        'L0_ffn_routed_w1', 'L0_ffn_routed_w2', 'L0_ffn_routed_w3']


def kernel(**inputs):
    import concourse.bacc as _bacc
    from concourse.bass_utils import run_bass_kernel_spmd as _run

    nc = _bacc.Bacc("TRN2", target_bir_lowering=False, num_devices=1)
    arrays, args = {}, []
    for name in _INS:
        a = np.ascontiguousarray(inputs[name])
        arrays[f"in_{name}_dram"] = a
        args.append(nc.dram_tensor(f"in_{name}_dram", a.shape, F32, kind="ExternalInput").ap())
    args.append(nc.dram_tensor("out_0_dram", (NB, P, D), F32, kind="ExternalOutput").ap())
    args.append(nc.dram_tensor("qk_parts", (3, 4, P, T), BF16, kind="Internal").ap())
    decoder_layer(nc, *args)
    r = _run(nc, [arrays], core_ids=[0])
    return r.results[0]["out_0_dram"]
```

```python
from contextlib import ExitStack

import numpy as np

import concourse.bass as bass
from concourse import mybir

ALU = mybir.AluOpType
ACT = mybir.ActivationFunctionType
F32 = mybir.dt.float32
BF16 = mybir.dt.bfloat16
I32 = mybir.dt.int32
U32 = mybir.dt.uint32
AX_X = mybir.AxisListType.X
ds = bass.ds

P = 128
NB, D = 16, 256
T = NB * P
KT = D // P
H, HD = 16, 8
NMAP = 2 * H
VD = 2 * HD
VP = 32
LAMBDA_INIT = 0.8 - 0.6 * float(np.exp(-0.3 * 12))
EPS = 1e-5
FLT_MAX = float(np.finfo(np.float32).max)
SQ_MAX = (FLT_MAX / VD) ** 0.5 * (1 - 2.0 ** -20)
SUM_MAX = FLT_MAX / VD ** 2
TEMPERATURE = 8.0
NE, RH, SH = 16, 256, 1024
NT = 2 * T // P + NE
CB = 4
NC = NB // CB
CT = CB * P
PAIRS = [(0, 0), (0, 1), (1, 0), (1, 1), (0, 2), (2, 0)]
KQ = len(PAIRS) * HD
KM = KQ + 3
START = 4096


class Line:

    def __init__(self, eng, sem, step=1, hold=None):
        self.eng, self.sem, self.step, self.hold = eng, sem, step, hold
        self.base, self.k = 0, 0

    def mark(self, ins):
        ins.then_inc(self.sem, self.step)
        self.k += self.step
        return (self, self.base, self.k)

    def last(self):
        return (self, self.base, self.k)

    def wait(self, *tokens):
        for line, base, k in tokens:
            self.eng.wait_ge(line.sem, base + k)
            if self.hold is not None and not isinstance(base, int):
                self.eng.sem_inc(self.hold, 1)

    def settle(self):
        self.wait(self.last())


class Count:

    def __init__(self, eng, sem, step=1):
        self.sem, self.step = sem, step
        eng.sem_inc(sem, START)

    def up(self, ins):
        ins.then_inc(self.sem, self.step)

    def at(self, n):
        return (self, n * self.step, START + self.step)


class Loop:

    def __init__(self, nc, n, lines, name):
        self.nc, self.n, self.lines, self.name, self.per = nc, n, lines, name, PER[name]

    def __enter__(self):
        self.cm = self.nc.Fori(0, self.n)
        self.i = self.cm.__enter__()
        self.outer = [(l.base, l.k) for l in self.lines]
        for l, per in zip(self.lines, self.per):
            l.base, l.k = self.i * per + (l.base + l.k), 0
        return self.i

    def __exit__(self, *exc):
        if exc[0] is None:
            got = [l.k for l in self.lines]
            assert got == self.per, f"{self.name} marks per iteration: {got}"
        r = self.cm.__exit__(*exc)
        for l, per, (base, k) in zip(self.lines, self.per, self.outer):
            l.base, l.k = base, k + per * self.n
        return r


def decoder_layer(nc, x, ctx_1024, W_qkv, W_proj, b_proj, lq1, lk1, lq2, lk2, subln_w,
                  Wq, bq, Wk, bk, Wv, bv, Wf, bf, router_w, expert_bias,
                  sw1, sw2, sw3, rw1, rw2, rw3, out, qk_parts, xT_all, x_slots, y_slots, upto=99, dbg=None):
    es = ExitStack()
    with es:
        def sb(name, shape, dt=F32, stack=es):
            return stack.enter_context(nc.sbuf_tensor(name, shape, dt))

        ps = es.enter_context(nc.psum_tensor("ps", [P, 8, 512], F32))

        def sem(name):
            return es.enter_context(nc.semaphore(name))

        V = Line(nc.vector, sem("done_vector"), hold=sem("hold_vector"))
        A = Line(nc.scalar, sem("done_scalar"))
        M = Line(nc.tensor, sem("done_tensor"))
        G = Line(nc.gpsimd, sem("done_gpsimd"), hold=sem("hold_gpsimd"))
        hold_sync = sem("hold_sync")
        Lw = Line(nc.sync, sem("loads_once"), 16, hold_sync)
        Lc = Line(nc.sync, sem("loads_of_chunk"), 16, hold_sync)
        Lm = Line(nc.sync, sem("loads_of_maxima"), 16, hold_sync)
        Lx = Line(nc.scalar, sem("loads_of_experts"), 16)
        Lz = Line(nc.scalar, sem("zeros_stored"), 16)
        Ls = Line(nc.gpsimd, sem("scattered"), 16)
        gathered = [Line(nc.gpsimd, sem(f"gathered{q}"), 16) for q in range(4)]
        lines = [V, A, M, G, Lw, Lc, Lm]
        turned, raised, flipped, lowered = (Count(nc.tensor, sem(n)) for n in ("turned", "raised", "flipped", "lowered"))
        xcopied, acted, hcopied = (Count(nc.scalar, sem(n)) for n in ("xcopied", "acted", "hcopied"))
        gated, yput = (Count(nc.vector, sem(n)) for n in ("gated", "yput"))
        fetched = [Count(nc.sync, sem(f"fetched{p}"), 16) for p in range(2)]
        stored = [Count(nc.scalar, sem(f"stored{p}"), 16) for p in range(2)]
        compute = [V, A, M, G]

        def join():
            marks = [l.last() for l in lines]
            for e in compute:
                e.wait(*marks)
            Lw.wait(*marks[:4])

        X = sb("X", [P, NB, D])
        ident = sb("ident", [P, P])
        identb = sb("identb", [P, P], BF16)
        st = sb("st", [P, CB, 6])
        mv = sb("mv", [P, CB, 2])
        rstd = sb("rstd", [P, CB])
        xn = sb("xn", [P, CB, D])
        xT = sb("xT", [P, KT, CT])
        va = sb("va", [P, 64])
        y = sb("y", [P, 64])
        t1 = sb("t1", [P, 64])
        bp_b = sb("bp_b", [P, D])
        bv_b = sb("bv_b", [P, D])
        bf_b = sb("bf_b", [P, D])
        bq_c = sb("bq_c", [P, KT])
        bk_c = sb("bk_c", [P, KT])
        sub_c = sb("sub_c", [P, 1])
        lam = sb("lam", [P, 4, HD])
        lw = sb("lw", [P, 8])
        neg_lam = sb("neg_lam", [P, 1])
        zero = sb("zero", [P, D])
        p2 = ExitStack()
        Wp = sb("Wp", [P, H // 4, D], F32, p2)
        WT = {n: sb("WT" + n, [P, KT, D], F32, p2) for n in ("q", "k", "v", "f")}
        Ob = sb("Ob", [P, NB, 4, 4, VD], F32, p2)

        def load(dst, src):
            return Lw.mark(nc.sync.dma_start(dst, src))

        def row(v, n):
            return v.rearrange("(o n) -> o n", o=1).to_broadcast([P, n])

        def inv_sqrt(v, n):
            yi = y[:, 0:n].bitcast(I32)
            V.mark(nc.vector.tensor_scalar(yi, v.bitcast(I32), 1, None, ALU.logical_shift_right))
            V.settle()
            V.mark(nc.vector.tensor_scalar(yi, yi, -1.0, float(0x5F3759DF), ALU.mult, ALU.add))
            V.settle()
            for _ in range(3):
                V.mark(nc.vector.tensor_tensor(t1[:, 0:n], y[:, 0:n], y[:, 0:n], ALU.mult))
                V.settle()
                V.mark(nc.vector.scalar_tensor_tensor(t1[:, 0:n], t1[:, 0:n], -0.5, v, ALU.mult, ALU.mult))
                V.settle()
                tok = V.mark(nc.vector.scalar_tensor_tensor(y[:, 0:n], t1[:, 0:n], 1.5, y[:, 0:n],
                                                            ALU.add, ALU.mult))
                V.settle()
            return tok

        def layernorm_T(c):
            for j in range(CB):
                V.mark(nc.vector.bn_stats(st[:, j, :], X[:, ds(c * CB + j, 1), :].rearrange("p o d -> p (o d)")))
            V.settle()
            for j in range(CB):
                V.mark(nc.vector.bn_aggr(mv[:, j, :], st[:, j, :]))
            V.settle()
            V.mark(nc.vector.tensor_scalar(va[:, 0:CB], mv[:, :, 1], EPS, None, ALU.add))
            V.settle()
            inv_sqrt(va[:, 0:CB], CB)
            copied = []
            for j in range(CB):
                n = V.mark(nc.vector.tensor_scalar(xn[:, j, :], X[:, ds(c * CB + j, 1), :].rearrange("p o d -> p (o d)"),
                                                   mv[:, j, 0:1], y[:, j:j + 1], ALU.subtract, ALU.mult))
                M.wait(n)
                if j >= 2:
                    M.wait(copied[j - 2])
                for k in range(KT):
                    r = nc.tensor.transpose(ps[:, j % 2, k * P:(k + 1) * P], xn[:, j, k * P:(k + 1) * P], ident[:, :])
                turned = M.mark(r)
                A.wait(turned)
                copied.append(A.mark(nc.scalar.activation(
                    xT[:, :, j * P:(j + 1) * P], ps[:, j % 2, 0:D].rearrange("p (k t) -> p k t", k=KT), ACT.Copy)))
            return copied

        for l in compute:
            l.eng.sem_inc(l.sem, START)
            l.k = START
        with nc.allow_non_contiguous_dma(reason="short vectors, once"):
            load(bq_c[:, :], bq.rearrange("(t p) -> p t", p=P))
            load(bk_c[:, :], bk.rearrange("(t p) -> p t", p=P))
        xv = x.rearrange("b p d -> p b d")
        for c in range(NC):
            load(X[:, c * CB:(c + 1) * CB, :], xv[:, c * CB:(c + 1) * CB, :])
        for dst, src, n in ((bp_b, b_proj, D), (bv_b, bv, D), (bf_b, bf, D)):
            load(dst[:, :], row(src, n))
        for i, v in enumerate((lq1, lk1, lq2, lk2)):
            load(lam[:, i, :], row(v, HD))
        A.wait(V.mark(nc.vector.memset(zero[:, :], 0.0)))
        for n in range(NT):
            Lz.mark(nc.scalar.dma_start(x_slots[n * P:(n + 1) * P, :], zero[:, :]))
        zeroed = V.mark(nc.vector.memset(Wp[:, :, :], 0.0))
        zeroed = V.mark(nc.vector.memset(sub_c[:, :], 0.0))
        Lw.wait(V.last())
        for j in range(4):
            load(Wp[32 * j:32 * j + VD, :, :], W_proj.rearrange("(a j d) n -> j d a n", j=4, d=VD)[j])
            load(sub_c[32 * j:32 * j + VD, :], subln_w.rearrange("(d o) -> d o", o=1))
        G.mark(nc.gpsimd.memset(ident[:, :], 0.0))
        G.settle()
        G.mark(nc.gpsimd.affine_select(out=ident[:, :], in_=ident[:, :], compare_op=ALU.not_equal, fill=1.0,
                                       base=0, pattern=[[-1, P]], channel_multiplier=1))
        V.wait(G.last())
        V.mark(nc.vector.tensor_copy(identb[:, :], ident[:, :]))

        p1 = ExitStack()
        Wqkv = sb("Wqkv", [P, KT, 3 * D], F32, p1)
        Vt = sb("Vt", [P, NB, H, VD], F32, p1)
        p0 = ExitStack()
        Wraw = sb("Wraw", [P, 4, KT, D], F32, p0)
        load(Wqkv[:, :, :], W_qkv.rearrange("(k p) n -> p k n", p=P))
        for i, w in enumerate((Wq, Wk, Wv, Wf)):
            load(Wraw[:, i, :, :], w.rearrange("(e p) d -> p e d", p=P))
        join()
        for i, n in enumerate(("q", "k", "v", "f")):
            for e in range(KT):
                for k in range(KT):
                    r = nc.tensor.transpose(ps[:, i, k * D + e * P:k * D + (e + 1) * P],
                                            Wraw[:, i, e, k * P:(k + 1) * P], ident[:, :])
            A.wait(M.mark(r))
            A.mark(nc.scalar.activation(WT[n][:, :, :], ps[:, i, :].rearrange("p (k e) -> p k e", k=KT), ACT.Copy))
        for i in range(2):
            V.mark(nc.vector.tensor_tensor(lam[:, 2 * i, :], lam[:, 2 * i, :], lam[:, 2 * i + 1, :], ALU.mult))
        V.settle()
        for i in range(2):
            V.mark(nc.vector.tensor_reduce(lw[:, i:i + 1], lam[:, 2 * i, :], AX_X, ALU.add))
        A.wait(V.last())
        A.mark(nc.scalar.activation(lw[:, 2:4], lw[:, 0:2], ACT.Exp))
        V.wait(A.last())
        V.mark(nc.vector.tensor_tensor(lw[:, 4:5], lw[:, 3:4], lw[:, 2:3], ALU.subtract))
        V.settle()
        V.mark(nc.vector.tensor_scalar(neg_lam[:, :], lw[:, 4:5], -LAMBDA_INIT, None, ALU.add))
        V.mark(nc.vector.tensor_scalar(Wp[:, :, :], Wp[:, :, :], sub_c[:, 0:1], 1.0 - LAMBDA_INIT,
                                       ALU.mult, ALU.mult))
        join()
        p0.close()

        with ExitStack() as s1:
            part = sb("part", [P, 3, 4, CT], BF16, s1)
            rest = sb("rest", [P, 2, CT], F32, s1)
            with Loop(nc, NC, lines, "qkv") as c:
                join()
                ready = layernorm_T(c)
                M.wait(ready[-1])
                first, third = {}, {}
                for f in range(4):
                    bank = 2 + f
                    for k in range(KT):
                        r = nc.tensor.matmul(ps[:, bank, :], Wqkv[:, k, f * P:(f + 1) * P], xT[:, k, :],
                                             start=(k == 0), stop=(k == KT - 1))
                    made = M.mark(r)
                    A.wait(made)
                    first[f] = A.mark(nc.scalar.activation(part[:, 0, f, :], ps[:, bank, :], ACT.Copy))
                    V.wait(first[f])
                    if f >= 2:
                        V.wait(third[f - 2])
                    V.mark(nc.vector.tensor_tensor(rest[:, f % 2, :], ps[:, bank, :], part[:, 0, f, :], ALU.subtract))
                    V.settle()
                    second = V.mark(nc.vector.tensor_copy(part[:, 1, f, :], rest[:, f % 2, :]))
                    G.wait(second)
                    third[f] = G.mark(nc.gpsimd.tensor_tensor(part[:, 2, f, :], rest[:, f % 2, :], part[:, 1, f, :],
                                                              ALU.subtract))
                vcopied = []
                for j in range(CB):
                    if j >= 2:
                        M.wait(vcopied[j - 2])
                    for k in range(KT):
                        r = nc.tensor.matmul(ps[:, 6 + j % 2, 0:D], xT[:, k, j * P:(j + 1) * P],
                                             Wqkv[:, k, 2 * D:3 * D], start=(k == 0), stop=(k == KT - 1))
                    A.wait(M.mark(r))
                    vcopied.append(A.mark(nc.scalar.activation(
                        Vt[:, ds(c * CB + j, 1), :, :].rearrange("p o h d -> p (o h d)"), ps[:, 6 + j % 2, 0:D], ACT.Copy)))
                for q in range(3):
                    Lc.wait((first[3], second, third[3])[q])
                    Lc.mark(nc.sync.dma_start(qk_parts[q, :, :, ds(c * CT, CT)].rearrange("f p t -> p f t"),
                                              part[:, q, :, :]))
            join()

        with ExitStack() as s2:
            packs = [[sb(f"pack_{n}{u}", [64, NMAP, 2 * P], BF16, s2) for u in range(2)] for n in "qk"]
            Qp, Kp = packs
            Vs = sb("Vs", [P, 2, H, VP], F32, s2)
            nmax = sb("nmax", [P, 2, NMAP], F32, s2)
            mrest = sb("mrest", [P, 2, NMAP], F32, s2)
            mpart = sb("mpart", [P, 2, 3 * NMAP], BF16, s2)
            mT = sb("mT", [3 * NMAP, 2, P], BF16, s2)
            prob = sb("prob", [P, 4, 512], F32, s2)
            OT = sb("OT", [P, 2, 1024], F32, s2)
            rden = sb("rden", [P, 2, 4, 2, 4], F32, s2)
            o2 = sb("o2", [P, 4, 4, VD], F32, s2)
            o1 = sb("o1", [P, 4, 4, VD], F32, s2)
            for u in range(2):
                V.mark(nc.vector.memset(Kp[u][32:64, :, :], 1.0))
            G.mark(nc.gpsimd.memset(Vs[:, :, :, :], 0.0))
            G.settle()
            G.mark(nc.gpsimd.memset(Vs[:, :, :, VD:VD + 1], 1.0))
            with Loop(nc, NC, lines, "attn") as c:
                join()
                landed = []
                for u in range(2):
                    for dst, f0, which in ((Qp, 0, 0), (Kp, 2, 1)):
                        for r, pr in enumerate(PAIRS):
                            src = qk_parts[pr[which], f0:f0 + 2, :, ds(c * CT + u * 2 * P, 2 * P)]
                            for f in range(2):
                                Lc.mark(nc.sync.dma_start(dst[u][r * HD:(r + 1) * HD, f * H:(f + 1) * H, :],
                                                          src[f].rearrange("(h d) t -> d h t", d=HD)))
                    landed.append(Lc.last())
                landed = [landed[1]] * 2
                maxed, mput, exped, pv_done, otr, vsd, comb = {}, {}, {}, {}, {}, {}, {}

                def scores(u, g):
                    lo = (u % 2) * P
                    M.wait(landed[u // 2])
                    n = u * 8 + g
                    if n >= 2:
                        M.wait(maxed[n - 2])
                    for m in range(4):
                        j = 4 * g + m
                        r = nc.tensor.matmul(ps[:, g % 2, m * P:(m + 1) * P], Qp[u // 2][0:KQ, j, lo:lo + P],
                                             Kp[u // 2][0:KQ, j, lo:lo + P], start=True, stop=True)
                    V.wait(M.mark(r))
                    maxed[n] = V.mark(nc.vector.tensor_reduce(
                        nmax[:, u % 2, 4 * g:4 * g + 4], ps[:, g % 2, :].rearrange("p (m t) -> p m t", m=4),
                        AX_X, ALU.max, negate=True))

                def put_max(u):
                    b, lo = u % 2, (u % 2) * P
                    if u >= 2:
                        V.wait(mput[u - 2][0])
                    V.settle()
                    V.mark(nc.vector.tensor_copy(mpart[:, b, 0:NMAP], nmax[:, b, :]))
                    V.settle()
                    V.mark(nc.vector.tensor_tensor(mrest[:, b, :], nmax[:, b, :], mpart[:, b, 0:NMAP], ALU.subtract))
                    V.settle()
                    V.mark(nc.vector.tensor_copy(mpart[:, b, NMAP:2 * NMAP], mrest[:, b, :]))
                    V.settle()
                    V.mark(nc.vector.tensor_tensor(mpart[:, b, 2 * NMAP:], mrest[:, b, :], mpart[:, b, NMAP:2 * NMAP],
                                                   ALU.subtract))
                    M.wait(V.last())
                    if u >= 1:
                        M.wait(mput[u - 1][1])
                    turned = M.mark(nc.tensor.transpose(ps[0:3 * NMAP, 7, 0:P // 2].bitcast(BF16), mpart[:, b, :],
                                                        identb[:, :]))
                    A.wait(turned)
                    if u >= 2:
                        A.wait(mput[u - 2][2])
                    copied = A.mark(nc.scalar.activation(mT[:, b, :], ps[0:3 * NMAP, 7, 0:P // 2].bitcast(BF16), ACT.Copy))
                    Lm.wait(copied)
                    for q in range(3):
                        put = Lm.mark(nc.sync.dma_start(Qp[u // 2][KQ + q:KQ + q + 1, :, lo:lo + P],
                                                        mT[q * NMAP:(q + 1) * NMAP, b, :]))
                    mput[u] = (turned, copied, put)

                def exps(u, g):
                    lo, n = (u % 2) * P, u * 8 + g
                    bank = 2 + n % 3
                    M.wait(mput[u][2])
                    if n >= 3:
                        M.wait(exped[n - 3])
                    for hh in range(2):
                        for m in range(2):
                            j = m * H + 2 * g + hh
                            r = nc.tensor.matmul(ps[:, bank, (2 * hh + m) * P:(2 * hh + m + 1) * P],
                                                 Kp[u // 2][0:KM, j, lo:lo + P], Qp[u // 2][0:KM, j, lo:lo + P],
                                                 start=True, stop=True)
                    A.wait(M.mark(r))
                    if n >= 4:
                        A.wait(pv_done[n - 4])
                    exped[n] = A.mark(nc.scalar.activation(prob[:, n % 4, :], ps[:, bank, :], ACT.Exp, scale=HD ** -0.5))

                def values(u):
                    if u >= 2:
                        G.wait(pv_done[(u - 2) * 8 + 7])
                    vsd[u] = G.mark(nc.gpsimd.tensor_copy(
                        Vs[:, u % 2, :, 0:VD], Vt[:, ds(c * CB + u, 1), :, :].rearrange("p o h d -> p (o h) d")))

                def pv(u, g):
                    n, bank = u * 8 + g, 5 + g // 4
                    M.wait(exped[n], vsd[u])
                    if u >= 1 and g % 4 == 0:
                        M.wait(otr[(u - 1, g // 4)])
                    for hh in range(2):
                        h = 2 * g + hh
                        q, col = 32 * (h % 4), (h // 4 % 2) * 2 * P
                        r = nc.tensor.matmul(ps[q:q + VP, bank, col:col + 2 * P], Vs[:, u % 2, h, :],
                                             prob[:, n % 4, hh * 2 * P:(hh + 1) * 2 * P], start=True, stop=True,
                                             tile_position=(0, q))
                    pv_done[n] = M.mark(r)

                def turn(u, half):
                    V.wait(pv_done[u * 8 + half * 4 + 3])
                    if u >= 2:
                        V.wait(comb[u - 2])
                    otr[(u, half)] = V.mark(nc.vector.transpose(OT[:, u % 2, half * 512:(half + 1) * 512],
                                                                ps[:, 5 + half, :]))

                def combine(u):
                    o = OT[:, u % 2, :].rearrange("p (a m k d) -> p a m k d", a=4, m=2, k=4)
                    if u >= 2:
                        V.wait(comb[u - 2])
                    V.settle()
                    rd = rden[:, u % 2, :, :, :]
                    for m in range(2):
                        V.mark(nc.vector.reciprocal(rd[:, :, m, :], o[:, :, m, :, VD]))
                    V.settle()
                    V.mark(nc.vector.tensor_scalar(rd[:, :, 1, :], rd[:, :, 1, :], neg_lam[:, 0:1], None, ALU.mult))
                    G.wait(V.last())

                    def by(m):
                        return rd[:, :, m, :].unsqueeze(3).to_broadcast([P, 4, 4, VD])
                    G.mark(nc.gpsimd.tensor_tensor(o1[:, :, :, :], o[:, :, 0, :, 0:VD], by(0), ALU.mult))
                    G.mark(nc.gpsimd.tensor_tensor(o2[:, :, :, :], o[:, :, 1, :, 0:VD], by(1), ALU.mult))
                    G.settle()
                    comb[u] = G.mark(nc.gpsimd.tensor_tensor(
                        Ob[:, ds(c * CB + u, 1), :, :, :].rearrange("p o a k d -> p (o a k d)"),
                        o1[:, :, :, :].rearrange("p a k d -> p (a k d)"),
                        o2[:, :, :, :].rearrange("p a k d -> p (a k d)"), ALU.add))
                    G.settle()

                LEAD = 4
                values(0)
                for g in range(8):
                    scores(0, g)
                put_max(0)
                for u in range(CB):
                    if u + 1 < CB:
                        values(u + 1)
                        for g in range(LEAD):
                            scores(u + 1, g)
                    for g in range(8):
                        exps(u, g)
                        if u + 1 < CB and g + LEAD < 8:
                            scores(u + 1, g + LEAD)
                        if g == 8 - LEAD and u + 1 < CB:
                            put_max(u + 1)
                        if g >= 1:
                            pv(u, g - 1)
                        if g == 4 + 1:
                            turn(u, 0)
                    pv(u, 7)
                    turn(u, 1)
                    combine(u)
            join()
        p1.close()
        if upto == 2:
            fin = Lw.mark(nc.sync.dma_start(dbg, Ob[:, :, :, :, :].rearrange("p b a k d -> p (b a k d)")))
            nc.sync.wait_ge(Lw.sem, Lw.k)
            return

        wts = ExitStack()

        def wt(name, shape):
            return wts.enter_context(nc.sbuf_tensor(name, shape, F32, side="right"))
        W12 = wt("W12", [P, NE, KT, 2 * RH])
        W3 = wt("W3", [P, NE, KT, D])
        for e in range(NE):
            for i, w in enumerate((rw1, rw2)):
                Lx.mark(nc.scalar.dma_start(W12[:, e, :, i * RH:(i + 1) * RH], w[e].rearrange("(k p) f -> p k f", p=P)))
            Lx.mark(nc.scalar.dma_start(W3[:, e, :, :], rw3[e].rearrange("(k p) d -> p k d", p=P)))

        with ExitStack() as s3:
            ONp = sb("ONp", [P, CB, 16, VP], F32, s3)
            sq = sb("sq", [P, CB * 16, VD], F32, s3)
            fits = sb("fits", [P, CB * 16], F32, s3)
            oT = sb("oT", [P, CB, 4, P], F32, s3)
            Cx = sb("Cx", [P, CB, D], F32, s3)
            cT = sb("cT", [P, KT, CT], F32, s3)
            qT = sb("qT", [P, KT, CT], F32, s3)
            kT = sb("kT", [P, KT, CT], F32, s3)
            vp = sb("vp", [P, CB, D], F32, s3)
            nm = sb("nm", [P, CB], F32, s3)
            den = sb("den", [P, CB], F32, s3)
            pr_ = sb("pr_", [P, CB, P], F32, s3)
            pT = sb("pT", [P, CB, P], F32, s3)
            coT = sb("coT", [P, CB, KT, P], F32, s3)
            fo = sb("fo", [P, CB, D], F32, s3)
            V.mark(nc.vector.memset(ONp[:, :, :, :], 0.0))
            cv = ctx_1024.rearrange("b p d -> p b d")
            with Loop(nc, NC, lines, "cross") as c:
                join()
                Lc.mark(nc.sync.dma_start(Cx[:, :, :], cv[:, ds(c * CB, CB), :]))
                o = Ob[:, ds(c * CB, CB), :, :, :].rearrange("p b a k d -> p (b a k) d")
                V.mark(nc.vector.tensor_scalar(sq[:, :, :], o, 1.0 / VD, SQ_MAX, ALU.mult, ALU.min))
                V.settle()
                V.mark(nc.vector.tensor_scalar(sq[:, :, :], sq[:, :, :], -SQ_MAX, None, ALU.max))
                A.wait(V.last())
                A.mark(nc.scalar.activation(sq[:, :, :], sq[:, :, :], ACT.Square))
                V.wait(A.last())
                V.mark(nc.vector.tensor_reduce(va[:, :], sq[:, :, :], AX_X, ALU.add))
                V.settle()
                V.mark(nc.vector.tensor_scalar(fits[:, :], va[:, :], SUM_MAX, None, ALU.is_le))
                V.mark(nc.vector.tensor_scalar(va[:, :], va[:, :], SUM_MAX, float(VD), ALU.min, ALU.mult))
                V.settle()
                V.mark(nc.vector.tensor_scalar(va[:, :], va[:, :], EPS, None, ALU.add))
                V.settle()
                inv_sqrt(va[:, :], 64)
                V.mark(nc.vector.tensor_tensor(y[:, :], y[:, :], fits[:, :], ALU.mult))
                V.settle()
                V.mark(nc.vector.tensor_tensor(ONp[:, :, :, 0:VD].rearrange("p b a d -> p (b a) d"), o,
                                               y[:, :].unsqueeze(2).to_broadcast([P, 64, VD]), ALU.mult))
                V.settle()
                o_turned = V.mark(nc.vector.transpose(oT[:, :, :, :].rearrange("p b a t -> p (b a t)"),
                                                    ONp[:, :, :, :].rearrange("p b a d -> p (b a d)")))
                M.wait(o_turned)
                for j in range(CB):
                    for a in range(4):
                        r = nc.tensor.matmul(ps[:, 2 + j, 0:D], oT[:, j, a, :], Wp[:, a, :],
                                             start=(a == 0), stop=(a == 3))
                    V.wait(M.mark(r))
                    xj = X[:, ds(c * CB + j, 1), :].rearrange("p o d -> p (o d)")
                    V.mark(nc.vector.tensor_tensor(xj, ps[:, 2 + j, 0:D], xj, ALU.add))
                V.settle()
                for j in range(CB):
                    xj = X[:, ds(c * CB + j, 1), :].rearrange("p o d -> p (o d)")
                    V.mark(nc.vector.tensor_tensor(xj, xj, bp_b[:, :], ALU.add))
                V.settle()
                M.wait(Lc.last())
                G.wait(Lc.last())
                cc = []
                for j in range(CB):
                    if j >= 2:
                        M.wait(cc[j - 2])
                    for k in range(KT):
                        r = nc.tensor.transpose(ps[:, 6 + j % 2, k * P:(k + 1) * P], Cx[:, j, k * P:(k + 1) * P],
                                                ident[:, :])
                    A.wait(M.mark(r))
                    cc.append(A.mark(nc.scalar.activation(
                        cT[:, :, j * P:(j + 1) * P], ps[:, 6 + j % 2, 0:D].rearrange("p (k t) -> p k t", k=KT),
                        ACT.Copy)))
                xr = layernorm_T(c)
                M.wait(cc[-1], xr[-1], V.last())
                for i, (dst, w, b, src) in enumerate(((kT, "k", bk_c, cT), (qT, "q", bq_c, xT))):
                    for e in range(KT):
                        for k in range(KT):
                            r = nc.tensor.matmul(ps[:, 2 + 2 * i + e, :], WT[w][:, k, e * P:(e + 1) * P], src[:, k, :],
                                                 start=(k == 0), stop=(k == KT - 1))
                        A.wait(M.mark(r))
                        A.mark(nc.scalar.activation(dst[:, e, :], ps[:, 2 + 2 * i + e, :], ACT.Identity, bias=b[:, e:e + 1]))
                qk_ready = A.last()
                vd = []
                for j in range(CB):
                    if j >= 2:
                        M.wait(vd[j - 2])
                    for k in range(KT):
                        r = nc.tensor.matmul(ps[:, 6 + j % 2, 0:D], cT[:, k, j * P:(j + 1) * P], WT["v"][:, k, :],
                                             start=(k == 0), stop=(k == KT - 1))
                    V.wait(M.mark(r))
                    vd.append(V.mark(nc.vector.tensor_tensor(vp[:, j, :], ps[:, 6 + j % 2, 0:D], bv_b[:, :], ALU.add)))
                M.wait(qk_ready)
                for j in range(CB):
                    for k in range(KT):
                        r = nc.tensor.matmul(ps[:, j, 0:P], qT[:, k, j * P:(j + 1) * P], kT[:, k, j * P:(j + 1) * P],
                                             start=(k == 0), stop=(k == KT - 1))
                    V.wait(M.mark(r))
                    V.mark(nc.vector.tensor_reduce(nm[:, j:j + 1], ps[:, j, 0:P], AX_X, ALU.max, negate=True))
                V.settle()
                V.mark(nc.vector.tensor_scalar(nm[:, :], nm[:, :], 1.0 / TEMPERATURE, None, ALU.mult))
                A.wait(V.last())
                for j in range(CB):
                    A.mark(nc.scalar.activation(pr_[:, j, :], ps[:, j, 0:P], ACT.Exp, scale=1.0 / TEMPERATURE,
                                                bias=nm[:, j:j + 1], accum_out=den[:, j:j + 1]))
                V.wait(A.last())
                V.mark(nc.vector.reciprocal(den[:, :], den[:, :]))
                V.settle()
                for j in range(CB):
                    V.mark(nc.vector.tensor_scalar(pr_[:, j, :], pr_[:, j, :], den[:, j:j + 1], None, ALU.mult))
                    M.wait(V.last())
                    A.wait(M.mark(nc.tensor.transpose(ps[:, 4, j * P:(j + 1) * P], pr_[:, j, :], ident[:, :])))
                tp = A.mark(nc.scalar.activation(pT[:, :, :].rearrange("p b t -> p (b t)"), ps[:, 4, :], ACT.Copy))
                M.wait(tp)
                for j in range(CB):
                    for e in range(KT):
                        r = nc.tensor.matmul(ps[:, j, e * P:(e + 1) * P], vp[:, j, e * P:(e + 1) * P], pT[:, j, :],
                                             start=True, stop=True)
                    A.wait(M.mark(r))
                    done = A.mark(nc.scalar.activation(coT[:, j, :, :].rearrange("p k t -> p (k t)"), ps[:, j, 0:D],
                                                       ACT.Copy))
                    M.wait(done)
                    for k in range(KT):
                        r = nc.tensor.matmul(ps[:, 4 + j, 0:D], coT[:, j, k, :], WT["f"][:, k, :],
                                             start=(k == 0), stop=(k == KT - 1))
                    V.wait(M.mark(r))
                    V.mark(nc.vector.tensor_tensor(fo[:, j, :], ps[:, 4 + j, 0:D], bf_b[:, :], ALU.add))
                A.wait(V.last())
                A.mark(nc.scalar.activation(fo[:, :, :], fo[:, :, :], ACT.Gelu))
                G.wait(A.last())
                G.mark(nc.gpsimd.tensor_tensor(fo[:, :, :], fo[:, :, :], Cx[:, :, :], ALU.add))
                G.settle()
                xc = X[:, ds(c * CB, CB), :]
                G.mark(nc.gpsimd.tensor_tensor(xc, xc, fo[:, :, :], ALU.add))
            join()
        if upto == 3:
            fin = Lw.mark(nc.sync.dma_start(dbg, X[:, :, :].rearrange("p b d -> p (b d)")))
            nc.sync.wait_ge(Lw.sem, Lw.k)
            return

        p2.close()
        with ExitStack() as s4:
            Wr = sb("Wr", [P, KT, NE], F32, s4)
            eb = sb("eb", [P, NE], F32, s4)
            XN = sb("XN", [P, NB, D], F32, s4)
            score = sb("score", [P, NB, NE], F32, s4)
            slot_i = sb("slot_i", [P, 2, NB], I32, s4)
            gate = sb("gate", [P, 2, NB], F32, s4)
            expert_of = sb("expert_of", [1, NT], I32, s4)
            W1s = sb("W1s", [P, KT, SH], F32, s4)
            W2s = sb("W2s", [P, KT, SH], F32, s4)
            W3s = sb("W3s", [P, SH // P, D], F32, s4)
            load(Wr[:, :, :], router_w.rearrange("(k p) e -> p k e", p=P))
            Lx.mark(nc.scalar.dma_start(W1s[:, :, :], sw1[0].rearrange("(k p) f -> p k f", p=P)))
            Lx.mark(nc.scalar.dma_start(W2s[:, :, :], sw2[0].rearrange("(k p) f -> p k f", p=P)))
            Lx.mark(nc.scalar.dma_start(W3s[:, :, :], sw3[0].rearrange("(f p) d -> p f d", p=P)))
            load(eb[:, :], row(expert_bias, NE))
            with Loop(nc, NC, lines, "router") as c:
                join()
                xr = layernorm_T(c)
                Lc.wait(xr[-1])
                Lc.mark(nc.sync.dma_start(xT_all[ds(c, 1), :, :, :].rearrange("o p k t -> p (o k) t"), xT[:, :, :]))
                Lc.mark(nc.sync.dma_start(XN[:, ds(c * CB, CB), :], xn[:, :, :]))
                M.wait(xr[-1])
                for j in range(CB):
                    for k in range(KT):
                        r = nc.tensor.matmul(ps[:, 2, j * NE:(j + 1) * NE], xT[:, k, j * P:(j + 1) * P], Wr[:, k, :],
                                             start=(k == 0), stop=(k == KT - 1))
                A.wait(M.mark(r))
                A.mark(nc.scalar.activation(score[:, ds(c * CB, CB), :].rearrange("p j e -> p (j e)"),
                                            ps[:, 2, 0:CB * NE], ACT.Sigmoid))
            join()

            with ExitStack() as sr:
                sel = sb("sel", [P, NB, NE], F32, sr)
                eq = sb("eq", [P, NB, NE], F32, sr)
                top = sb("top", [P, NB], F32, sr)
                first = sb("first", [P, NB, NE], F32, sr)
                second = sb("second", [P, NB, NE], F32, sr)
                both = sb("both", [P, NB, NE], F32, sr)
                before = sb("before", [P, NB + 1, NE], F32, sr)
                back = sb("back", [P, NE], F32, sr)
                ones = sb("ones", [P, P], F32, sr)
                earlier = sb("earlier", [P, P], F32, sr)
                e_less = sb("e_less", [P, NE, NE], F32, sr)
                tile_no = sb("tile_no", [P, NT], F32, sr)
                tiles = sb("tiles", [P, NE], F32, sr)
                tiles_i = sb("tiles_i", [P, NE], I32, sr)
                first_tile = sb("first_tile", [P, NE], F32, sr)
                end_tile = sb("end_tile", [P, NE], F32, sr)
                ended = sb("ended", [P, NT, NE], F32, sr)
                slot = sb("slot", [P, NB, NE], F32, sr)
                G.mark(nc.gpsimd.iota(back[:, :], pattern=[[-1, NE]], base=NE, channel_multiplier=0,
                                      allow_small_or_imprecise_dtypes=True))
                G.mark(nc.gpsimd.iota(e_less[:, :, :], pattern=[[1, NE], [-1, NE]], base=0, channel_multiplier=0,
                                      allow_small_or_imprecise_dtypes=True))
                G.mark(nc.gpsimd.iota(tile_no[:, :], pattern=[[1, NT]], base=0, channel_multiplier=0,
                                      allow_small_or_imprecise_dtypes=True))
                G.mark(nc.gpsimd.memset(ones[:, :], 1.0))
                G.mark(nc.gpsimd.memset(earlier[:, :], 1.0))
                G.settle()
                G.mark(nc.gpsimd.affine_select(out=earlier[:, :], in_=earlier[:, :], compare_op=ALU.is_gt, fill=0.0,
                                               base=0, pattern=[[1, P]], channel_multiplier=-1))
                V.wait(G.last())

                def vec(ins):
                    V.mark(ins)
                    V.settle()

                def wide(v):
                    return v[:, :].unsqueeze(1).to_broadcast([P, NB, NE])

                def per_token(v):
                    return v.unsqueeze(2).to_broadcast([P, NB, NE])

                def flat(v):
                    return v[:, :, :].rearrange("p j e -> p (j e)")
                vec(nc.vector.tensor_tensor(sel[:, :, :], score[:, :, :], wide(eb), ALU.add))
                for chosen in (first, second):
                    vec(nc.vector.tensor_reduce(top[:, :], sel[:, :, :], AX_X, ALU.max))
                    vec(nc.vector.tensor_tensor(eq[:, :, :], sel[:, :, :], per_token(top[:, :]), ALU.is_equal))
                    vec(nc.vector.tensor_tensor(eq[:, :, :], eq[:, :, :], wide(back), ALU.mult))
                    vec(nc.vector.tensor_reduce(top[:, :], eq[:, :, :], AX_X, ALU.max))
                    vec(nc.vector.tensor_tensor(chosen[:, :, :], eq[:, :, :], per_token(top[:, :]), ALU.is_equal))
                    if chosen is first:
                        vec(nc.vector.scalar_tensor_tensor(flat(sel), flat(chosen), -3.0e38, flat(sel), ALU.mult, ALU.add))
                vec(nc.vector.tensor_tensor(both[:, :, :], first[:, :, :], second[:, :, :], ALU.add))
                vec(nc.vector.memset(before[:, 0, :], 0.0))
                for b in range(NB):
                    vec(nc.vector.tensor_tensor(before[:, b + 1, :], before[:, b, :], both[:, b, :], ALU.add))
                M.wait(V.last())
                nc.tensor.matmul(ps[:, 0, 0:NB * NE], earlier[:, :], flat(both), start=True, stop=False)
                nc.tensor.matmul(ps[:, 0, 0:NB * NE], ones[:, :], before[:, 0:NB, :].rearrange("p b e -> p (b e)"),
                                 start=False, stop=True)
                V.wait(M.mark(nc.tensor.matmul(ps[:, 1, 0:NE], ones[:, :], before[:, NB, :], start=True, stop=True)))
                vec(nc.vector.tensor_scalar(tiles_i[:, :], ps[:, 1, 0:NE], float(P - 1), None, ALU.add))
                vec(nc.vector.tensor_scalar(tiles_i[:, :], tiles_i[:, :], 7, None, ALU.logical_shift_right))
                vec(nc.vector.tensor_copy(tiles[:, :], tiles_i[:, :]))
                vec(nc.vector.tensor_scalar(e_less[:, :, :], e_less[:, :, :], 0.0, None, ALU.is_gt))
                vec(nc.vector.tensor_tensor(e_less[:, :, :], e_less[:, :, :],
                                            tiles[:, :].unsqueeze(1).to_broadcast([P, NE, NE]), ALU.mult))
                vec(nc.vector.tensor_reduce(first_tile[:, :], e_less[:, :, :], AX_X, ALU.add))
                vec(nc.vector.tensor_tensor(end_tile[:, :], first_tile[:, :], tiles[:, :], ALU.add))
                vec(nc.vector.tensor_scalar(first_tile[:, :], first_tile[:, :], float(P), None, ALU.mult))
                vec(nc.vector.tensor_tensor(slot[:, :, :], ps[:, 0, 0:NB * NE].rearrange("p (b e) -> p b e", b=NB),
                                            wide(first_tile), ALU.add))
                for i, chosen in enumerate((first, second)):
                    vec(nc.vector.tensor_tensor(eq[:, :, :], slot[:, :, :], chosen[:, :, :], ALU.mult))
                    vec(nc.vector.tensor_reduce(top[:, :], eq[:, :, :], AX_X, ALU.add))
                    vec(nc.vector.tensor_copy(slot_i[:, i, :], top[:, :]))
                G.wait(V.last())
                G.wait(Lz.last())
                for i in range(2):
                    for b in range(NB):
                        Ls.mark(nc.gpsimd.indirect_dma_start(
                            out=x_slots, out_offset=bass.IndirectOffsetOnAxis(ap=slot_i[:, i, b:b + 1].bitcast(U32), axis=0),
                            in_=XN[:, b, :], in_offset=None))
                for i, chosen in enumerate((first, second)):
                    vec(nc.vector.tensor_tensor(eq[:, :, :], score[:, :, :], chosen[:, :, :], ALU.mult))
                    vec(nc.vector.tensor_reduce(gate[:, i, :], eq[:, :, :], AX_X, ALU.add))
                vec(nc.vector.tensor_tensor(ended[0:1, :, :], end_tile[0:1, :].unsqueeze(1).to_broadcast([1, NT, NE]),
                                            tile_no[0:1, :].unsqueeze(2).to_broadcast([1, NT, NE]), ALU.is_le))
                vec(nc.vector.tensor_reduce(tile_no[0:1, :], ended[0:1, :, :], AX_X, ALU.add))
                vec(nc.vector.tensor_scalar(expert_of[0:1, :], tile_no[0:1, :], float(NE - 1), None, ALU.min))
            join()

            hTs = sb("hTs", [P, SH // P, CT], F32, s4)
            sil = sb("sil", [P, 2, CT], F32, s4)
            for e in compute:
                e.wait(Lx.last())

            def shared(c):
                join()
                Lc.mark(nc.sync.dma_start(xT[:, :, :], xT_all[ds(c, 1), :, :, :].rearrange("o p k t -> p (o k) t")))
                M.wait(Lc.last())
                had = {}
                for f in range(SH // P):
                    if f >= 2:
                        M.wait(had[f - 2])
                    for w, bank in ((W1s, 2 * (f % 2)), (W2s, 2 * (f % 2) + 1)):
                        for k in range(KT):
                            r = nc.tensor.matmul(ps[:, bank, :], w[:, k, f * P:(f + 1) * P], xT[:, k, :],
                                                 start=(k == 0), stop=(k == KT - 1))
                    A.wait(M.mark(r))
                    V.wait(A.mark(nc.scalar.activation(sil[:, f % 2, :], ps[:, 2 * (f % 2), :], ACT.Silu)))
                    had[f] = V.mark(nc.vector.tensor_tensor(hTs[:, f, :], sil[:, f % 2, :], ps[:, 2 * (f % 2) + 1, :],
                                                            ALU.mult))
                    if f >= 2:
                        pass
                M.wait(had[SH // P - 1])
                for j in range(CB):
                    for f in range(SH // P):
                        r = nc.tensor.matmul(ps[:, 4 + j, 0:D], hTs[:, f, j * P:(j + 1) * P], W3s[:, f, :],
                                             start=(f == 0), stop=(f == SH // P - 1))
                    V.wait(M.mark(r))
                    xj = X[:, ds(c * CB + j, 1), :].rearrange("p o d -> p (o d)")
                    V.mark(nc.vector.tensor_tensor(xj, ps[:, 4 + j, 0:D], xj, ALU.add))

            with Loop(nc, NC // 2, lines, "shared") as c:
                shared(c)
            join()

            xg = sb("xg", [P, 2, D], F32, s4)
            xt = sb("xt", [P, 2, KT, P], F32, s4)
            sa = sb("sa", [P, 2, RH], F32, s4)
            ht = sb("ht", [P, 2, KT, P], F32, s4)
            yo = sb("yo", [P, 2, D], F32, s4)
            for e in (nc.sync, nc.tensor):
                e.wait_ge(Ls.sem, Ls.k)

            def turn_x(n, p):
                Lc.wait(turned.at(n - 2))
                fetched[p].up(nc.sync.dma_start(xg[:, p, :], x_slots[ds(n * P, P), :]))
                M.wait(fetched[p].at((n - p) // 2), xcopied.at(n - 2))
                for k in range(KT):
                    r = nc.tensor.transpose(ps[:, p, k * P:(k + 1) * P], xg[:, p, k * P:(k + 1) * P], ident[:, :])
                turned.up(r)
                A.wait(turned.at(n), raised.at(n - 2))
                xcopied.up(nc.scalar.activation(xt[:, p, :, :].rearrange("p k t -> p (k t)"), ps[:, p, 0:D], ACT.Copy))

            def raise_(n, p):
                e = nc.tensor.value_load(expert_of[0:1, ds(n, 1)], min_val=0, max_val=NE - 1)
                M.wait(xcopied.at(n), gated.at(n - 2))
                for k in range(KT):
                    r = nc.tensor.matmul(ps[:, 2 + p, :], xt[:, p, k, :],
                                         W12[:, ds(e, 1), k, :].rearrange("p o f -> p (o f)"),
                                         start=(k == 0), stop=(k == KT - 1))
                raised.up(r)
                A.wait(raised.at(n), flipped.at(n - 2))
                acted.up(nc.scalar.activation(sa[:, p, :], ps[:, 2 + p, 0:RH], ACT.Silu))
                V.wait(acted.at(n))
                gated.up(nc.vector.tensor_tensor(sa[:, p, :], sa[:, p, :], ps[:, 2 + p, RH:2 * RH], ALU.mult))

            def flip(n, p):
                M.wait(gated.at(n), hcopied.at(n - 2))
                for k in range(KT):
                    r = nc.tensor.transpose(ps[:, 4 + p, k * P:(k + 1) * P], sa[:, p, k * P:(k + 1) * P], ident[:, :])
                flipped.up(r)
                A.wait(flipped.at(n), lowered.at(n - 2))
                hcopied.up(nc.scalar.activation(ht[:, p, :, :].rearrange("p k t -> p (k t)"), ps[:, 4 + p, 0:D], ACT.Copy))

            def lower(n, p):
                e = nc.tensor.value_load(expert_of[0:1, ds(n, 1)], min_val=0, max_val=NE - 1)
                M.wait(hcopied.at(n), yput.at(n - 2))
                for k in range(KT):
                    r = nc.tensor.matmul(ps[:, 6 + p, 0:D], ht[:, p, k, :],
                                         W3[:, ds(e, 1), k, :].rearrange("p o f -> p (o f)"),
                                         start=(k == 0), stop=(k == KT - 1))
                lowered.up(r)
                V.wait(lowered.at(n), stored[p].at((n - p) // 2 - 1))
                yput.up(nc.vector.tensor_copy(yo[:, p, :], ps[:, 6 + p, 0:D]))
                A.wait(yput.at(n))
                stored[p].up(nc.scalar.dma_start(y_slots[ds(n * P, P), :], yo[:, p, :]))

            turn_x(0, 0)
            turn_x(1, 1)
            raise_(0, 0)
            turn_x(2, 0)
            raise_(1, 1)
            flip(0, 0)
            with nc.Fori(0, (NT - 4) // 2) as i:
                for j in range(2):
                    turn_x(i * 2 + (3 + j), (1 + j) % 2)
                    raise_(i * 2 + (2 + j), j)
                    flip(i * 2 + (1 + j), (1 + j) % 2)
                    lower(i * 2 + j, j)
            n = NT - 3
            turn_x(n + 2, (n + 2) % 2)
            for n in range(NT - 3, NT + 1):
                for part, m in ((raise_, n + 1), (flip, n), (lower, n - 1)):
                    if m < NT:
                        part(m, m % 2)

            yg = sb("yg", [P, 4, D], F32, s4)
            G.wait(stored[0].at(NT // 2 - 1), stored[1].at(NT // 2 - 1))
            with Loop(nc, NC // 2, lines, "shared") as c:
                shared(c + NC // 2)
            join()
            added = {}
            for b in range(NB):
                for i in range(2):
                    q = (2 * b + i) % 4
                    if b >= 2:
                        G.wait(added[(b - 2, i)])
                    got = gathered[q].mark(nc.gpsimd.indirect_dma_start(
                        out=yg[:, q, :], out_offset=None, in_=y_slots,
                        in_offset=bass.IndirectOffsetOnAxis(ap=slot_i[:, i, b:b + 1].bitcast(U32), axis=0)))
                    V.wait(got)
                    if i == 1:
                        V.settle()
                    added[(b, i)] = V.mark(nc.vector.scalar_tensor_tensor(
                        X[:, b, :], yg[:, q, :], gate[:, i, b:b + 1], X[:, b, :], ALU.mult, ALU.add))
                if b % CB == CB - 1:
                    Lc.wait(V.last())
                    Lc.mark(nc.sync.dma_start(out.rearrange("b p d -> p b d")[:, b + 1 - CB:b + 1, :],
                                              X[:, b + 1 - CB:b + 1, :]))
            nc.sync.wait_ge(Lc.sem, Lc.base + Lc.k)
            join()
        wts.close()


PER = {
    "qkv": [32, 12, 12, 4, 0, 48, 0],
    "attn": [68, 36, 100, 16, 0, 768, 192],
    "cross": [70, 23, 36, 2, 0, 16, 0],
    "router": [24, 5, 5, 0, 0, 32, 0],
    "shared": [12, 8, 12, 0, 0, 16, 0],
}

_INS = ['x', 'ctx_1024', 'L0_attn_W_qkv', 'L0_attn_W_proj', 'L0_attn_b_proj', 'L0_attn_lambda_q1',
        'L0_attn_lambda_k1', 'L0_attn_lambda_q2', 'L0_attn_lambda_k2', 'L0_attn_subln_w', 'L0_xattn_Wq',
        'L0_xattn_bq', 'L0_xattn_Wk', 'L0_xattn_bk', 'L0_xattn_Wv', 'L0_xattn_bv', 'L0_xattn_Wf', 'L0_xattn_bf',
        'L0_ffn_router_w', 'L0_ffn_expert_bias', 'L0_ffn_shared_w1', 'L0_ffn_shared_w2', 'L0_ffn_shared_w3',
        'L0_ffn_routed_w1', 'L0_ffn_routed_w2', 'L0_ffn_routed_w3']


def scratch(nc):
    return [nc.dram_tensor("qk_parts", (3, 4, P, T), BF16, kind="Internal").ap(),
            nc.dram_tensor("xT_all", (NC, P, KT, CT), F32, kind="Internal").ap(),
            nc.dram_tensor("x_slots", (NT * P, D), F32, kind="Internal").ap(),
            nc.dram_tensor("y_slots", (NT * P, D), F32, kind="Internal").ap()]


def kernel(**inputs):
    import concourse.bacc as _bacc
    from concourse.bass_utils import run_bass_kernel_spmd as _run

    nc = _bacc.Bacc("TRN2", target_bir_lowering=False, num_devices=1)
    arrays, args = {}, []
    for name in _INS:
        a = np.ascontiguousarray(inputs[name])
        arrays[f"in_{name}_dram"] = a
        args.append(nc.dram_tensor(f"in_{name}_dram", a.shape, F32, kind="ExternalInput").ap())
    args.append(nc.dram_tensor("out_0_dram", (NB, P, D), F32, kind="ExternalOutput").ap())
    args += scratch(nc)
    decoder_layer(nc, *args)
    r = _run(nc, [arrays], core_ids=[0])
    return r.results[0]["out_0_dram"]
```

```python
from contextlib import ExitStack

import numpy as np

import concourse.bass as bass
from concourse import mybir

ALU = mybir.AluOpType
ACT = mybir.ActivationFunctionType
F32 = mybir.dt.float32
BF16 = mybir.dt.bfloat16
I32 = mybir.dt.int32
U32 = mybir.dt.uint32
AX_X = mybir.AxisListType.X
ds = bass.ds

P = 128
NB, D = 16, 256
T = NB * P
KT = D // P
H, HD = 16, 8
NMAP = 2 * H
VD = 2 * HD
VP = 32
LAMBDA_INIT = 0.8 - 0.6 * float(np.exp(-0.3 * 12))
EPS = 1e-5
FLT_MAX = float(np.finfo(np.float32).max)
SQ_MAX = (FLT_MAX / VD) ** 0.5 * (1 - 2.0 ** -20)
SUM_MAX = FLT_MAX / VD ** 2
TEMPERATURE = 8.0
NE, RH, SH = 16, 256, 1024
NT = 2 * T // P + NE
ZT, EL = 4, 4
CB = 4
NC = NB // CB
CT = CB * P
PAIRS = [(0, 0), (1, 1), (0, 2), (0, 1), (1, 0), (2, 0)]
Q_RUNS = [(0, 0, 2), (2, 0, 1), (3, 0, 3)]
K_RUNS = [(0, 0, 3), (3, 1, 1), (4, 0, 1), (5, 0, 1)]
FETCHES = len(Q_RUNS) + len(K_RUNS) + 1
HU = H // 2
MU = 2 * HU
UNITS, LEAD = 4, 3
KQ = len(PAIRS) * HD
KM = KQ + 3
START = 4096


class Line:

    def __init__(self, eng, sem, step=1, hold=None):
        self.eng, self.sem, self.step, self.hold = eng, sem, step, hold
        self.base, self.k = 0, 0

    def mark(self, ins):
        ins.then_inc(self.sem, self.step)
        self.k += self.step
        return (self, self.base, self.k)

    def last(self):
        return (self, self.base, self.k)

    def wait(self, *tokens):
        for line, base, k in tokens:
            self.eng.wait_ge(line.sem, base + k)
            if self.hold is not None and not isinstance(base, int):
                self.eng.sem_inc(self.hold, 1)

    def settle(self):
        self.wait(self.last())


class Count:

    def __init__(self, eng, sem, step=1, inc=None):
        self.sem, self.step, self.inc = sem, step, inc or step
        eng.sem_inc(sem, START)

    def up(self, ins):
        ins.then_inc(self.sem, self.inc)

    def at(self, n):
        return (self, n * self.step, START + self.step)


class Loop:

    def __init__(self, nc, n, lines, name):
        self.nc, self.n, self.lines, self.name, self.per = nc, n, lines, name, PER[name]

    def __enter__(self):
        self.cm = self.nc.Fori(0, self.n)
        self.i = self.cm.__enter__()
        self.outer = [(l.base, l.k) for l in self.lines]
        for l, per in zip(self.lines, self.per):
            l.base, l.k = self.i * per + (l.base + l.k), 0
        return self.i

    def __exit__(self, *exc):
        if exc[0] is None:
            got = [l.k for l in self.lines]
            assert got == self.per, f"{self.name} marks per iteration: {got}"
        r = self.cm.__exit__(*exc)
        for l, per, (base, k) in zip(self.lines, self.per, self.outer):
            l.base, l.k = base, k + per * self.n
        return r


def decoder_layer(nc, x, ctx_1024, W_qkv, W_proj, b_proj, lq1, lk1, lq2, lk2, subln_w,
                  Wq, bq, Wk, bk, Wv, bv, Wf, bf, router_w, expert_bias,
                  sw1, sw2, sw3, rw1, rw2, rw3, out, qk_parts, xT_all, x_slots, y_slots):
    es = ExitStack()
    with es:
        def sb(name, shape, dt=F32, stack=es):
            return stack.enter_context(nc.sbuf_tensor(name, shape, dt))

        ps = es.enter_context(nc.psum_tensor("ps", [P, 8, 512], F32))

        def sem(name):
            return es.enter_context(nc.semaphore(name))

        V = Line(nc.vector, sem("done_vector"), hold=sem("hold_vector"))
        A = Line(nc.scalar, sem("done_scalar"))
        M = Line(nc.tensor, sem("done_tensor"))
        G = Line(nc.gpsimd, sem("done_gpsimd"), hold=sem("hold_gpsimd"))
        hold_sync = sem("hold_sync")
        Lw = Line(nc.sync, sem("loads_once"), 16, hold_sync)
        Lc = Line(nc.sync, sem("loads_of_chunk"), 16, hold_sync)
        Lm = Line(nc.sync, sem("loads_of_maxima"), 16, hold_sync)
        Lx = Line(nc.scalar, sem("loads_of_experts"), 16)
        Lz = Line(nc.sync, sem("zeros_stored"), 16)
        Lr = Line(nc.sync, sem("loads_of_routed"), 16)
        Lxt = [Line(nc.sync, sem(f"xT_of_chunk{c}"), 16) for c in range(NC)]
        cleared, cleared_vs = sem("cleared"), sem("cleared_values")
        Lv = Line(nc.sync, sem("context_loaded"), 16)
        Lf = Line(nc.sync, sem("first_chunk_loaded"), 16)
        Lg = Line(nc.sync, sem("W_qkv_loaded"), 16)
        Lb = Line(nc.sync, sem("loads_for_later"), 16)
        out_stored = sem("out_stored")
        Ls = Line(nc.gpsimd, sem("scattered"), 16)
        gathered = [Line(nc.gpsimd, sem(f"gathered{q}"), 16) for q in range(2)]
        lines = [V, A, M, G, Lw, Lc, Lm]
        turned, raised, flipped, lowered = (Count(nc.tensor, sem(n)) for n in ("turned", "raised", "flipped", "lowered"))
        xcopied, acted, hcopied = (Count(nc.scalar, sem(n)) for n in ("xcopied", "acted", "hcopied"))
        gated, yput = (Count(nc.vector, sem(n)) for n in ("gated", "yput"))
        fetched = [Count(nc.sync, sem(f"fetched{p}"), 16) for p in range(2)]
        stored = [Count(nc.scalar, sem(f"stored{p}"), 16) for p in range(2)]
        compute = [V, A, M, G]

        def join(but=()):
            marks = [l.last() for l in lines if l not in but]
            for e in compute:
                e.wait(*marks)
            Lw.wait(*marks[:4])

        X = sb("X", [P, NB, D])
        ident = sb("ident", [P, P])
        identb = sb("identb", [P, P], BF16)
        va = sb("va", [P, 64])
        newton = sb("newton", [P, 64])
        minus_half = sb("minus_half", [P, 64])
        bq_c = sb("bq_c", [P, KT])
        bk_c = sb("bk_c", [P, KT])
        sub_c = sb("sub_c", [P, 1])
        lam = sb("lam", [P, 4, HD])
        lw = sb("lw", [P, 8])
        neg_lam = sb("neg_lam", [P, 1])

        def load(dst, src):
            return Lw.mark(nc.sync.dma_start(dst, src))

        def later(dst, src):
            return Lb.mark(nc.sync.dma_start(dst, src))

        def row(v, n):
            return v.rearrange("(o n) -> o n", o=1).to_broadcast([P, n])

        def inv_sqrt(y, v, n):
            G.wait(V.last())
            G.mark(nc.gpsimd.tensor_scalar(y[:, 0:n], v, EPS, None, ALU.add))
            G.settle()
            return G.mark(nc.gpsimd.tensor_tensor(y[:, 0:n], y[:, 0:n], minus_half[:, 0:n], ALU.pow))

        def inv_sqrt_v(y, v, n):
            yi = y[:, 0:n].bitcast(I32)
            t = newton[:, 0:n]
            V.settle()
            V.mark(nc.vector.tensor_scalar(v, v, EPS, None, ALU.add))
            V.settle()
            V.mark(nc.vector.tensor_scalar(yi, v.bitcast(I32), 1, None, ALU.logical_shift_right))
            V.settle()
            V.mark(nc.vector.tensor_scalar(yi, yi, -1.0, float(0x5F3759DF), ALU.mult, ALU.add))
            V.settle()
            for _ in range(3):
                V.mark(nc.vector.tensor_tensor(t, y, y, ALU.mult))
                V.settle()
                V.mark(nc.vector.scalar_tensor_tensor(t, t, -0.5, v, ALU.mult, ALU.mult))
                V.settle()
                V.mark(nc.vector.scalar_tensor_tensor(y, t, 1.5, y, ALU.add, ALU.mult))
                V.settle()
            return V.last()

        class Norm:

            def __init__(self, name, stack_sb, bank):
                self.st = stack_sb("st" + name, [P, CB, 6])
                self.mv = stack_sb("mv" + name, [P, CB, 2])
                self.y = stack_sb("y" + name, [P, CB])
                self.xn = stack_sb("xn" + name, [P, CB, D])
                self.xT = stack_sb("xT" + name, [P, KT, CT])
                self.bank = bank

            def stats(self, c):
                for j in range(CB):
                    V.mark(nc.vector.bn_stats(self.st[:, j, :], X[:, ds(c * CB + j, 1), :].rearrange("p o d -> p (o d)")))
                V.settle()
                for j in range(CB):
                    V.mark(nc.vector.bn_aggr(self.mv[:, j, :], self.st[:, j, :]))
                self.scaled = inv_sqrt(self.y, self.mv[:, :, 1], CB)

            def normalize(self, c):
                V.wait(self.scaled)
                self.normed = [V.mark(nc.vector.tensor_scalar(
                    self.xn[:, j, :], X[:, ds(c * CB + j, 1), :].rearrange("p o d -> p (o d)"),
                    self.mv[:, j, 0:1], self.y[:, j:j + 1], ALU.subtract, ALU.mult)) for j in range(CB)]

            def turn(self):
                for j in range(CB):
                    M.wait(self.normed[j])
                    for k in range(KT):
                        lo = (j % 2 * KT + k) * P
                        r = nc.tensor.transpose(ps[:, self.bank + j // 2, lo:lo + P], self.xn[:, j, k * P:(k + 1) * P],
                                                ident[:, :])
                    if j % 2:
                        A.wait(M.mark(r))
                        A.mark(nc.scalar.activation(
                            self.xT[:, :, (j - 1) * P:(j + 1) * P].rearrange("p k (j t) -> p k j t", j=2),
                            ps[:, self.bank + j // 2, :].rearrange("p (j k t) -> p k j t", j=2, k=KT), ACT.Copy))
                return A.last()

        norm = Norm("", sb, 0)
        xT = norm.xT
        p2 = ExitStack()
        Wp = sb("Wp", [P, 2, D], F32, p2)
        WT = {n: sb("WT" + n, [P, KT, D], F32, p2) for n in ("q", "k", "v", "f")}
        Cx = sb("Cx", [P, NB, D], F32, p2)
        bp_b = sb("bp_b", [P, D], F32, p2)
        bv_b = sb("bv_b", [P, D], F32, p2)
        bf_b = sb("bf_b", [P, D], F32, p2)
        zero = sb("zero", [P, D], F32, p2)
        fits = sb("fits", [P, CB * 16], F32, p2)
        yo_ = sb("yo_", [P, CB * 16], F32, p2)
        sq = sb("sq", [P, CB * 16, VD], F32, p2)
        Ob = sb("Ob", [P, NB, 2, 4, 2, VD], F32, p2)

        p1 = ExitStack()
        Wqkv = sb("Wqkv", [P, KT, 3 * D], F32, p1)
        Vt = sb("Vt", [P, NB, H, VD], F32, p1)
        Wqk = sb("Wqk", [P, KT, 4, HD, MU], F32, p1)
        Wraw = sb("Wraw", [P, 4, KT, D], F32, p1)
        s2 = ExitStack()
        Qp, Kp = ([sb(f"pack_{n}{u}", [P, MU, 2 * P], BF16, s2) for u in range(UNITS)] for n in "qk")
        constant = sb("constant", [3, 2, 2 * P], BF16, s2)

        for l in compute:
            l.eng.sem_inc(l.sem, START)
            l.k = START
        xv = x.rearrange("b p d -> p b d")
        x_first = Lf.mark(nc.sync.dma_start(X[:, 0:CB, :], xv[:, 0:CB, :]))
        W_first = Lg.mark(nc.sync.dma_start(Wqkv[:, :, :], W_qkv.rearrange("(k p) n -> p k n", p=P)))
        for c in range(1, NC):
            load(X[:, c * CB:(c + 1) * CB, :], xv[:, c * CB:(c + 1) * CB, :])
        with nc.allow_non_contiguous_dma(reason="short vectors, once"):
            later(bq_c[:, :], bq.rearrange("(t p) -> p t", p=P))
            later(bk_c[:, :], bk.rearrange("(t p) -> p t", p=P))
        for dst, src, n in ((bp_b, b_proj, D), (bv_b, bv, D), (bf_b, bf, D)):
            later(dst[:, :], row(src, n))
        for i, v in enumerate((lq1, lk1, lq2, lk2)):
            later(lam[:, i, :], row(v, HD))
        V.mark(nc.vector.memset(zero[:, :], 0.0))
        V.mark(nc.vector.memset(minus_half[:, :], -0.5))
        for j in range(4):
            for i in range(2):
                r0 = 32 * j + VD * i
                later(Wp[r0:r0 + VD, :, :], W_proj.rearrange("(a i j d) n -> i j d a n", i=2, j=4, d=VD)[i, j])
                later(sub_c[r0:r0 + VD, :], subln_w.rearrange("(d o) -> d o", o=1))
        G.mark(nc.gpsimd.memset(ident[:, :], 0.0))
        G.settle()
        G.mark(nc.gpsimd.affine_select(out=ident[:, :], in_=ident[:, :], compare_op=ALU.not_equal, fill=1.0,
                                       base=0, pattern=[[-1, P]], channel_multiplier=1))
        V.wait(G.last())
        V.mark(nc.vector.tensor_copy(identb[:, :], ident[:, :]))

        for i, w in enumerate((Wq, Wk, Wv, Wf)):
            later(Wraw[:, i, :, :], w.rearrange("(e p) d -> p e d", p=P))
        Lz.wait(V.last())
        V.wait(x_first)
        norm.stats(0)
        norm.normalize(0)
        norm.turn()
        V.wait(W_first)
        for f in range(4):
            for k in range(KT):
                for m in range(2):
                    c0 = f // 2 * D + m * P + f % 2 * HU * HD
                    V.mark(nc.vector.tensor_copy(Wqk[:, k, f, :, m * HU:(m + 1) * HU],
                                                 Wqkv[:, k, c0:c0 + HU * HD].rearrange("p (h d) -> p d h", d=HD)))
        Vs = sb("Vs", [P, 4, HU, VP], F32, s2)
        nmax = sb("nmax", [P, 4, MU], F32, s2)
        mrest = sb("mrest", [P, 4, MU], F32, s2)
        mpart = sb("mpart", [P, 4, P], BF16, s2)
        mT = sb("mT", [P, 4, P], BF16, s2)
        OT = sb("OT", [P, 2, 512], F32, s2)
        rden = sb("rden", [P, 2, 4, 4], F32, s2)
        o12 = sb("o12", [P, 2, 2, 4 * VD], F32, s2)
        def rows(t, c):
            return t[:, ds(c * CB, CB), :]

        def attn_of(c):
            return Ob[:, ds(c * CB, CB), :, :, :, :].rearrange("p b a k i d -> p (b a k i) d")

        def square_o(c):
            V.mark(nc.vector.tensor_scalar(sq[:, :, :], attn_of(c), 1.0 / VD, SQ_MAX, ALU.mult, ALU.min))
            V.settle()
            V.mark(nc.vector.tensor_scalar(sq[:, :, :], sq[:, :, :], -SQ_MAX, None, ALU.max))
            A.wait(V.last())
            return A.mark(nc.scalar.activation(sq[:, :, :], sq[:, :, :], ACT.Square))

        def scale_o(c, squared, on_vector=False):
            V.wait(squared)
            V.mark(nc.vector.tensor_reduce(va[:, :], sq[:, :, :], AX_X, ALU.add))
            V.settle()
            V.mark(nc.vector.tensor_scalar(fits[:, :], va[:, :], SUM_MAX, None, ALU.is_le))
            V.mark(nc.vector.tensor_scalar(va[:, :], va[:, :], SUM_MAX, float(VD), ALU.min, ALU.mult))
            scaled = (inv_sqrt_v if on_vector else inv_sqrt)(yo_[:, :], va[:, :], CB * 16)
            G.mark(nc.gpsimd.tensor_tensor(rows(X, c), rows(X, c),
                                           bp_b[:, :].unsqueeze(1).to_broadcast([P, CB, D]), ALU.add))
            return scaled

        n_cleared = [0]

        def clear(ins):
            ins.then_inc(cleared, 1)
            n_cleared[0] += 1

        clear(nc.vector.memset(constant[:, 0, :], 0.0))
        clear(nc.vector.memset(constant[:, 1, :], 1.0))
        for u in range(UNITS):
            for n, t in enumerate((Qp[u], Kp[u])):
                if 2 * u + n < 3:
                    clear(nc.vector.memset(t[:, :, :].bitcast(F32), 0.0))
                else:
                    clear(nc.gpsimd.memset(t[:, :, :].bitcast(F32), 0.0))
        clear(nc.vector.memset(mpart[:, :, :], 0.0))
        nc.gpsimd.memset(Vs[:, :, :, :], 0.0).then_inc(cleared_vs, 1)
        nc.gpsimd.wait_ge(cleared_vs, 1)
        clear(nc.gpsimd.memset(Vs[:, :, :, VD:VD + 1], 1.0))
        nc.sync.wait_ge(cleared, n_cleared[0])
        for u in range(UNITS):
            later(Kp[u][KQ:KM, :, :], constant[:, 1, :].unsqueeze(1).to_broadcast([3, MU, 2 * P]))
        scored, m_turned, s_done, pv_done = (Count(nc.tensor, sem(n))
                                             for n in ("scored", "max_turned", "s_done", "pv_done"))
        packed = [Count(nc.sync, sem(f"packed{u}"), 16 * FETCHES, 16) for u in range(UNITS)]

        def q_side(u, half):
            return [(Qp[u], half, Q_RUNS)]

        def k_side(u, half):
            return [(Kp[u], 2 + half, K_RUNS)]

        def fetch(i, k, bufs):
            n, half = i * 2 + k // 2, k % 2
            Lw.wait(s_done.at((i * 4 + (k - UNITS)) * 8 + 7))
            u = k % UNITS
            for buf, f, runs in bufs(u, half):
                for r0, p0, np_ in runs:
                    packed[u].up(nc.sync.dma_start(
                        buf[r0 * HD:(r0 + np_) * HD, :, :].rearrange("p m t -> p (m t)"),
                        qk_parts[ds(n, 1), f, p0:p0 + np_, :, :, :].rearrange("o q d m t -> (o q d) (m t)")))
            if bufs is q_side:
                packed[u].up(nc.sync.dma_start(Qp[u][KQ:KM, :, :], constant[:, 0, :].unsqueeze(1).to_broadcast([3, MU, 2 * P])))

        with ExitStack() as s1:
            part = sb("part", [P, 3, 4, CT], BF16, s1)
            rest = sb("rest", [P, 2, CT], F32, s1)
            def qkv(c, more=True):
                if more:
                    norm.stats(c + 1)
                first, third = {}, {}
                for f in range(4):
                    bank = 2 + f
                    for k in range(KT):
                        r = nc.tensor.matmul(ps[:, bank, :], Wqk[:, k, f, :, :].rearrange("p d m -> p (d m)"), xT[:, k, :],
                                             start=(k == 0), stop=(k == KT - 1))
                    made = M.mark(r)
                    A.wait(made)
                    if f == 0:
                        for e in (A, V, G):
                            e.wait(Lc.last())
                    first[f] = A.mark(nc.scalar.activation(part[:, 0, f, :], ps[:, bank, :], ACT.Copy))
                    V.wait(first[f])
                    if f >= 2:
                        V.wait(third[f - 2])
                    V.mark(nc.vector.tensor_tensor(rest[:, f % 2, :], ps[:, bank, :], part[:, 0, f, :], ALU.subtract))
                    V.settle()
                    second = V.mark(nc.vector.tensor_copy(part[:, 1, f, :], rest[:, f % 2, :]))
                    G.wait(second)
                    third[f] = G.mark(nc.gpsimd.tensor_tensor(part[:, 2, f, :], rest[:, f % 2, :], part[:, 1, f, :],
                                                              ALU.subtract))
                    if more and f == 1:
                        norm.normalize(c + 1)
                vcopied = []
                for j in range(CB):
                    if j >= 2:
                        M.wait(vcopied[j - 2])
                    for k in range(KT):
                        r = nc.tensor.matmul(ps[:, 6 + j % 2, 0:D], xT[:, k, j * P:(j + 1) * P],
                                             Wqkv[:, k, 2 * D:3 * D], start=(k == 0), stop=(k == KT - 1))
                    A.wait(M.mark(r))
                    vcopied.append(A.mark(nc.scalar.activation(
                        Vt[:, ds(c * CB + j, 1), :, :].rearrange("p o h d -> p (o h d)"), ps[:, 6 + j % 2, 0:D], ACT.Copy)))
                if more:
                    norm.turn()
                for q in range(3):
                    Lc.wait((first[3], second, third[3])[q])
                    for n in range(2):
                        Lc.mark(nc.sync.dma_start(
                            qk_parts[ds(c * 2 + n, 1), :, q, :, :, :].rearrange("o f d m t -> (o d m) f t"),
                            part[:, q, :, n * 2 * P:(n + 1) * 2 * P]))

            with Loop(nc, NC - 1, lines, "qkv") as c:
                join(but=[Lc])
                qkv(c)
            join(but=[Lc])
            Lw.wait(Lc.last(), Lb.last())
            for k in range(UNITS):
                fetch(0, k, q_side)
                if k < UNITS - 1:
                    fetch(0, k, k_side)
            qkv(NC - 1, more=False)
            join(but=[Lc])

        with s2:
            maxed, o_turned, inverted = (Count(nc.vector, sem(n)) for n in ("maxed", "o_turned", "inverted"))
            mcopied, exped = (Count(nc.scalar, sem(n)) for n in ("max_copied", "exped"))
            chained, parted, valued, weighed, combined = (Count(nc.gpsimd, sem(n)) for n in
                                                          ("chained", "parted", "valued", "weighed", "combined"))
            mput = [Count(nc.sync, sem(f"max_put{q}"), 16) for q in range(4)]

            prob = sb("prob", [P, 8, 512], F32, s2)
            Lw.wait(Lc.last())

            def scores(i, j):
                u, lo = j // 2 % UNITS, (j % 2) * P
                for g in range(4):
                    n = (i * 8 + j) * 4 + g
                    M.wait(*([packed[u].at(i + j // 8)] if g == 0 else []), maxed.at(n - 2))
                    for m in range(4):
                        r = nc.tensor.matmul(ps[:, g % 2, m * P:(m + 1) * P], Qp[u][:, 4 * g + m, lo:lo + P],
                                             Kp[u][:, 4 * g + m, lo:lo + P], start=True, stop=True)
                    scored.up(r)
                    V.wait(*([parted.at(i * 8 + (j - 4))] if g == 0 else []), scored.at(n))
                    maxed.up(nc.vector.tensor_reduce(nmax[:, j % 4, 4 * g:4 * g + 4],
                                                     ps[:, g % 2, :].rearrange("p (m t) -> p m t", m=4),
                                                     AX_X, ALU.max, negate=True))
                    yield

            def split_max(i, j):
                q, s = j % 4, i * 8 + j
                G.wait(maxed.at(s * 4 + 3), m_turned.at(s - 4))
                chained.up(nc.gpsimd.tensor_copy(mpart[:, q, 0:MU], nmax[:, q, :]))
                G.wait(chained.at(s * 3))
                chained.up(nc.gpsimd.tensor_tensor(mrest[:, q, :], nmax[:, q, :], mpart[:, q, 0:MU], ALU.subtract))
                G.wait(chained.at(s * 3 + 1))
                chained.up(nc.gpsimd.tensor_copy(mpart[:, q, MU:2 * MU], mrest[:, q, :]))
                G.wait(chained.at(s * 3 + 2))
                parted.up(nc.gpsimd.tensor_tensor(mpart[:, q, 2 * MU:3 * MU], mrest[:, q, :], mpart[:, q, MU:2 * MU],
                                                  ALU.subtract))

            def turn_max(i, j):
                q, u, lo, s = j % 4, j // 2 % UNITS, (j % 2) * P, i * 8 + j
                M.wait(parted.at(s), mcopied.at(s - 1))
                m_turned.up(nc.tensor.transpose(ps[:, 7, 0:P // 2].bitcast(BF16), mpart[:, q, :], identb[:, :]))
                A.wait(m_turned.at(s), mput[q].at(i * 2 + (j // 4 - 1)))
                mcopied.up(nc.scalar.activation(mT[:, q, :], ps[:, 7, 0:P // 2].bitcast(BF16), ACT.Copy))
                Lw.wait(mcopied.at(s))
                mput[q].up(nc.sync.dma_start(Qp[u][KQ:KM, :, lo:lo + P], mT[0:3 * MU, q, :]))

            def exps(i, j, g):
                u, lo, s = j // 2 % UNITS, (j % 2) * P, i * 8 + j
                n = s * 4 + g
                M.wait(*([mput[j % 4].at(i * 2 + j // 4)] if g == 0 else []), exped.at(n - 2))
                for hh in range(2):
                    for m in range(2):
                        k = m * HU + 2 * g + hh
                        r = nc.tensor.matmul(ps[:, 2 + g % 2, (2 * hh + m) * P:(2 * hh + m + 1) * P],
                                             Kp[u][:, k, lo:lo + P], Qp[u][:, k, lo:lo + P], start=True, stop=True)
                s_done.up(r)
                A.wait(s_done.at(n), pv_done.at(s * 2 + (g // 2 - 4)))
                exped.up(nc.scalar.activation(prob[:, (j % 2) * 4 + g, :], ps[:, 2 + g % 2, :], ACT.Exp,
                                              scale=HD ** -0.5))

            def values(i, j):
                h0, s = (j // 2 % 2) * HU, i * 8 + j
                G.wait(pv_done.at(s * 2 - 7))
                valued.up(nc.gpsimd.tensor_copy(
                    Vs[:, j % 4, :, 0:VD],
                    Vt[:, ds(i * 4 + (j // 4 * 2 + j % 2), 1), h0:h0 + HU, :].rearrange("p o h d -> p (o h) d")))

            def pv(i, j, a):
                s = i * 8 + j
                M.wait(exped.at(s * 4 + (2 * a + 1)), valued.at(s), o_turned.at(s - 2))
                for h in range(4):
                    r = nc.tensor.matmul(ps[VP * h:VP * (h + 1), 5 + j % 2, a * 2 * P:(a + 1) * 2 * P],
                                         Vs[:, j % 4, 4 * a + h, :],
                                         prob[:, (j % 2) * 4 + 2 * a + h // 2, h % 2 * 2 * P:(h % 2 + 1) * 2 * P],
                                         start=True, stop=True, tile_position=(0, VP * h))
                pv_done.up(r)

            def turn_o(i, j):
                p, s = j % 2, i * 8 + j
                V.wait(pv_done.at(s * 2 + 1), combined.at(s - 2))
                o_turned.up(nc.vector.transpose(OT[:, p, :], ps[:, 5 + p, :]))

            def invert(i, j):
                p, s = j % 2, i * 8 + j
                V.wait(o_turned.at(s))
                inverted.up(nc.vector.reciprocal(rden[:, p, :, :],
                                                 OT[:, p, :].rearrange("p (a k d) -> p a k d", a=4, k=4)[:, :, :, VD]))

            def combine(i, j):
                p, half, s = j % 2, j // 2 % 2, i * 8 + j
                o = OT[:, p, :].rearrange("p (a m k d) -> p a m k d", a=2, m=2, k=4)
                rd = rden[:, p, :, :].rearrange("p (a m) k -> p a m k", a=2)
                G.wait(inverted.at(s))
                weighed.up(nc.gpsimd.tensor_scalar(rd[:, :, 1, :], rd[:, :, 1, :], neg_lam[:, 0:1], None, ALU.mult))
                G.wait(weighed.at(s * 2))
                for m in range(2):
                    r = nc.gpsimd.tensor_tensor(o12[:, m, :, :].rearrange("p a (k d) -> p a k d", k=4),
                                                o[:, :, m, :, 0:VD],
                                                rd[:, :, m, :].unsqueeze(3).to_broadcast([P, 2, 4, VD]), ALU.mult)
                weighed.up(r)
                G.wait(weighed.at(s * 2 + 1))
                combined.up(nc.gpsimd.tensor_tensor(
                    Ob[:, ds(i * 4 + (j // 4 * 2 + j % 2), 1), half, :, :, :].rearrange("p o k i d -> p i (o k) d"),
                    o12[:, 0, :, :].rearrange("p i (k d) -> p i k d", d=VD),
                    o12[:, 1, :, :].rearrange("p i (k d) -> p i k d", d=VD), ALU.add))

            def step(i, j, left=LEAD):
                ahead = scores(i, j + LEAD) if left >= LEAD else None
                first_step = j == 0
                if left >= LEAD - 1:
                    split_max(i, j + LEAD - 1)
                if left >= 1:
                    values(i, j + 1)
                for g in range(4):
                    exps(i, j, g)
                    if ahead:
                        next(ahead)
                    if g == 0 and not first_step:
                        pv(i, j - 1, 1)
                        turn_o(i, j - 1)
                    if g == 1 and not first_step:
                        invert(i, j - 1)
                        combine(i, j - 1)
                    if g == 2:
                        pv(i, j, 0)
                        if left >= LEAD - 1:
                            turn_max(i, j + LEAD - 1)

            def prepare_weights():
                for e in compute:
                    e.wait(Lb.last())
                for i, n in enumerate(("q", "k", "v", "f")):
                    if i == 3:
                        M.wait(A.last())
                    for e in range(KT):
                        for k in range(KT):
                            r = nc.tensor.transpose(ps[:, 4 + i % 3, k * D + e * P:k * D + (e + 1) * P],
                                                    Wraw[:, i, e, k * P:(k + 1) * P], ident[:, :])
                    A.wait(M.mark(r))
                    A.mark(nc.scalar.activation(WT[n][:, :, :], ps[:, 4 + i % 3, :].rearrange("p (k e) -> p k e", k=KT), ACT.Copy))
                for i in range(2):
                    V.mark(nc.vector.tensor_tensor(lam[:, 2 * i, :], lam[:, 2 * i, :], lam[:, 2 * i + 1, :], ALU.mult))
                V.settle()
                for i in range(2):
                    V.mark(nc.vector.tensor_reduce(lw[:, i:i + 1], lam[:, 2 * i, :], AX_X, ALU.add))
                A.wait(V.last())
                A.mark(nc.scalar.activation(lw[:, 2:4], lw[:, 0:2], ACT.Exp))
                V.wait(A.last())
                V.mark(nc.vector.tensor_tensor(lw[:, 4:5], lw[:, 3:4], lw[:, 2:3], ALU.subtract))
                V.settle()
                V.mark(nc.vector.tensor_scalar(neg_lam[:, :], lw[:, 4:5], -LAMBDA_INIT, None, ALU.add))
                V.mark(nc.vector.tensor_scalar(Wp[:, :, :], Wp[:, :, :], sub_c[:, 0:1], 1.0 - LAMBDA_INIT,
                                               ALU.mult, ALU.mult))
                M.wait(A.last())
                G.wait(V.last())

            values(0, 0)
            for j in range(LEAD):
                for _ in scores(0, j):
                    pass
                if j == 0:
                    prepare_weights()
                if j < LEAD - 1:
                    split_max(0, j)
                if j >= 1:
                    turn_max(0, j - 1)
            A.wait(Lc.last())
            step(0, 0)
            STEPS = 2 * NB
            with nc.Fori(0, STEPS // 8 - 1) as i:
                for j in range(1, 9):
                    step(i, j)
                    fetch(i, j // 2 + UNITS - 1, k_side if j % 2 else q_side)
            for s in range(STEPS - 7, STEPS):
                step(STEPS // 8 - 1, s % 8, min(LEAD, STEPS - 1 - s))
                if s == STEPS - 4:
                    V.wait(combined.at(CB * 2 - 1))
                    squared = square_o(0)
                elif s == STEPS - 2:
                    scaled = scale_o(0, squared, on_vector=True)
                if s < STEPS - 7 + NC:
                    c = s - (STEPS - 7)
                    Lv.mark(nc.sync.dma_start(Cx[:, c * CB:(c + 1) * CB, :],
                                              ctx_1024.rearrange("b p d -> p b d")[:, c * CB:(c + 1) * CB, :]))
                if s == STEPS - 7:
                    fetch(STEPS // 8 - 1, UNITS - 1, k_side)
            last = (STEPS // 8 - 1, 7)
            pv(*last, 1)
            turn_o(*last)
            invert(*last)
            combine(*last)
            for e in compute + [Lw]:
                e.wait(combined.at(STEPS - 1))
        p1.close()

        wts = ExitStack()

        def wt(name, shape):
            return wts.enter_context(nc.sbuf_tensor(name, shape, F32, side="right"))
        W1s = wt("W1s", [P, KT, SH])
        W2s = wt("W2s", [P, KT, SH])
        W3s = wt("W3s", [P, SH // P, D])
        XN = wt("XN", [P, NB, D])
        score = wt("score", [P, NB, NE])
        Wr = wt("Wr", [P, KT, NE])
        eb = wt("eb", [P, NE])
        norm3 = Norm("3", wt, 6)
        load(Wr[:, :, :], router_w.rearrange("(k p) e -> p k e", p=P))
        load(eb[:, :], row(expert_bias, NE))
        Lx.mark(nc.scalar.dma_start(W1s[:, :, :], sw1[0].rearrange("(k p) f -> p k f", p=P)))
        Lx.mark(nc.scalar.dma_start(W2s[:, :, :], sw2[0].rearrange("(k p) f -> p k f", p=P)))
        Lx.mark(nc.scalar.dma_start(W3s[:, :, :], sw3[0].rearrange("(f p) d -> p f d", p=P)))

        for n in range(0, NT, ZT):
            Lz.mark(nc.sync.dma_start(x_slots[n * P:(n + ZT) * P, :].rearrange("(n p) d -> p n d", p=P),
                                        zero[:, :].unsqueeze(1).to_broadcast([P, ZT, D])))

        def route_store(c, turned):
            Lc.wait(turned)
            Lc.mark(nc.sync.dma_start(xT_all[ds(c, 1), :, :, :].rearrange("o p k t -> p (o k) t"), norm3.xT[:, :, :]))
            Lc.mark(nc.sync.dma_start(XN[:, ds(c * CB, CB), :], norm3.xn[:, :, :]))

        def route_logits(c, bank=1):
            for j in range(CB):
                for k in range(KT):
                    r = nc.tensor.matmul(ps[:, bank, j * NE:(j + 1) * NE], norm3.xT[:, k, j * P:(j + 1) * P], Wr[:, k, :],
                                         start=(k == 0), stop=(k == KT - 1))
            V.wait(M.mark(r))
            V.mark(nc.vector.tensor_copy(score[:, ds(c * CB, CB), :].rearrange("p j e -> p (j e)"), ps[:, bank, 0:CB * NE]))

        with ExitStack() as s3:
            On = sb("On", [P, CB * 16, VD], F32, s3)
            oT = sb("oT", [P, CB, 2, P], F32, s3)
            xc = sb("xc", [P, CB, D], F32, s3)
            cT = sb("cT", [P, KT, CT], F32, s3)
            qT = sb("qT", [P, KT, CT], F32, s3)
            kT = sb("kT", [P, KT, CT], F32, s3)
            vp = sb("vp", [P, CB, D], F32, s3)
            nm = sb("nm", [P, CB], F32, s3)
            den = sb("den", [P, CB], F32, s3)
            pr_ = sb("pr_", [P, CB, P], F32, s3)
            pT = sb("pT", [P, CB, P], F32, s3)
            coT = sb("coT", [P, CB, KT * P], F32, s3)
            fo = xc

            def wide2(v):
                return v[:, :].unsqueeze(1).to_broadcast([P, 2, D])

            def norm_o(c, scaled):
                V.wait(scaled)
                V.mark(nc.vector.tensor_tensor(yo_[:, :], yo_[:, :], fits[:, :], ALU.mult))
                V.settle()
                V.mark(nc.vector.tensor_tensor(On[:, :, :], attn_of(c), yo_[:, :].unsqueeze(2).to_broadcast([P, 64, VD]),
                                               ALU.mult))
                V.settle()
                return V.mark(nc.vector.transpose(oT[:, :, :, :].rearrange("p b a t -> p (b a t)"),
                                                  On[:, :, :].rearrange("p b d -> p (b d)")))

            def turn_context(c):
                A.mark(nc.scalar.activation(xc[:, :, :], rows(Cx, c), ACT.Copy))
                M.wait(A.last())
                for j in range(CB):
                    for k in range(KT):
                        r = nc.tensor.transpose(ps[:, 6 + j // 2, (j % 2 * KT + k) * P:(j % 2 * KT + k + 1) * P],
                                                xc[:, j, k * P:(k + 1) * P], ident[:, :])
                    if j % 2:
                        A.wait(M.mark(r))
                        A.mark(nc.scalar.activation(
                            cT[:, :, (j - 1) * P:(j + 1) * P].rearrange("p k (j t) -> p k j t", j=2),
                            ps[:, 6 + j // 2, :].rearrange("p (j k t) -> p k j t", j=2, k=KT), ACT.Copy))
                return A.last()

            def project_T(dst, w, bias, src, bank):
                done = []
                for e in range(KT):
                    for k in range(KT):
                        r = nc.tensor.matmul(ps[:, bank + e, :], WT[w][:, k, e * P:(e + 1) * P], src[:, k, :],
                                             start=(k == 0), stop=(k == KT - 1))
                    done.append(M.mark(r))

                def put():
                    for e in range(KT):
                        A.wait(done[e])
                        A.mark(nc.scalar.activation(dst[:, e, :], ps[:, bank + e, :], ACT.Identity, bias=bias[:, e:e + 1]))
                    return A.last()
                return put

            def project(w, src, bank):
                done = []
                for j in range(CB):
                    for k in range(KT):
                        r = nc.tensor.matmul(ps[:, bank + j // 2, j % 2 * D:(j % 2 + 1) * D], src(j, k), w(k),
                                             start=(k == 0), stop=(k == KT - 1))
                    if j % 2:
                        done.append(M.mark(r))
                return done

            def add_to(dst, done, bank, other):
                for i in range(2):
                    V.wait(done[i])
                    tok = V.mark(nc.vector.tensor_tensor(
                        dst(i), ps[:, bank + i, :].rearrange("p (j d) -> p j d", j=2), other(i), ALU.add))
                return tok

            def project_values():
                return project(lambda k: WT["v"][:, k, :], lambda j, k: cT[:, k, j * P:(j + 1) * P], 2)

            def put_values(done):
                return add_to(lambda i: vp[:, 2 * i:2 * i + 2, :], done, 2, lambda i: wide2(bv_b))

            def project_o():
                return project(lambda a: Wp[:, a, :], lambda j, a: oT[:, j, a, :], 2)

            def cross(c, more=True, route=True):
                if more:
                    context_turned = turn_context(c + 1)
                for i in range(2):
                    xi = X[:, ds(c * CB + 2 * i, 2), :]
                    x_added = V.mark(nc.vector.tensor_tensor(
                        xi, ps[:, 2 + i, :].rearrange("p (j d) -> p j d", j=2), xi, ALU.add))
                V.wait(x_added)
                norm.stats(c)
                norm.normalize(c)
                x_normed = V.last()
                if more:
                    M.wait(context_turned, x_added)
                    put_keys = project_T(kT, "k", bk_c, cT, 2)
                x_turned = norm.turn()
                if route:
                    norm3.stats(c - 1)
                G.wait(x_normed)
                context_added = G.mark(nc.gpsimd.tensor_tensor(rows(X, c), rows(X, c), rows(Cx, c), ALU.add))
                if more:
                    squared = square_o(c + 1)
                if route:
                    norm3.normalize(c - 1)
                M.wait(x_turned)
                q_ready = project_T(qT, "q", bq_c, xT, 4)()
                if more:
                    scaled = scale_o(c + 1, squared)
                if route:
                    route_turned = norm3.turn()
                    route_store(c - 1, route_turned)
                M.wait(q_ready)
                for j in range(CB):
                    for k in range(KT):
                        r = nc.tensor.matmul(ps[:, 0, j * P:(j + 1) * P], qT[:, k, j * P:(j + 1) * P],
                                             kT[:, k, j * P:(j + 1) * P], start=(k == 0), stop=(k == KT - 1))
                scores_done = M.mark(r)
                V.wait(scores_done)
                V.mark(nc.vector.tensor_reduce(nm[:, :], ps[:, 0, :].rearrange("p (j t) -> p j t", j=CB),
                                               AX_X, ALU.max, negate=True))
                V.settle()
                shift = V.mark(nc.vector.tensor_scalar(nm[:, :], nm[:, :], 1.0 / TEMPERATURE, None, ALU.mult))
                if more:
                    A.wait(scores_done)
                    keys_put = put_keys()
                if route:
                    M.wait(route_turned)
                    route_logits(c - 1)
                if more:
                    M.wait(keys_put)
                    values_done = project_values()
                A.wait(shift)
                for j in range(CB):
                    A.mark(nc.scalar.activation(pr_[:, j, :], ps[:, 0, j * P:(j + 1) * P], ACT.Exp,
                                                scale=1.0 / TEMPERATURE, bias=nm[:, j:j + 1], accum_out=den[:, j:j + 1]))
                V.wait(A.last())
                V.mark(nc.vector.reciprocal(den[:, :], den[:, :]))
                V.settle()
                for j in range(CB):
                    V.mark(nc.vector.tensor_scalar(pr_[:, j, :], pr_[:, j, :], den[:, j:j + 1], None, ALU.mult))
                    M.wait(V.last())
                    r = nc.tensor.transpose(ps[:, 4, j * P:(j + 1) * P], pr_[:, j, :], ident[:, :])
                A.wait(M.mark(r))
                M.wait(A.mark(nc.scalar.activation(pT[:, :, :].rearrange("p b t -> p (b t)"), ps[:, 4, :], ACT.Copy)))
                for j in range(CB):
                    for e in range(KT):
                        lo = (j % 2 * KT + e) * P
                        r = nc.tensor.matmul(ps[:, 6 + j // 2, lo:lo + P], vp[:, j, e * P:(e + 1) * P], pT[:, j, :],
                                             start=True, stop=True)
                    if j % 2:
                        A.wait(M.mark(r))
                        A.mark(nc.scalar.activation(coT[:, j - 1:j + 1, :].rearrange("p j t -> p (j t)"),
                                                    ps[:, 6 + j // 2, :], ACT.Copy))
                contexts, contexts_done = A.last(), M.last()
                if more:
                    V.wait(contexts_done)
                    values_put = put_values(values_done)
                    o_normed = norm_o(c + 1, scaled)
                M.wait(contexts)
                fed = project(lambda k: WT["f"][:, k, :], lambda j, k: coT[:, j, k * P:(k + 1) * P], 4)
                if more:
                    M.wait(values_put, o_normed)
                    project_o()
                added = add_to(lambda i: fo[:, 2 * i:2 * i + 2, :], fed, 4, lambda i: wide2(bf_b))
                V.wait(context_added)
                A.wait(added)
                for i in range(2):
                    A.mark(nc.scalar.activation(fo[:, 2 * i:2 * i + 2, :], fo[:, 2 * i:2 * i + 2, :], ACT.Gelu))
                    V.wait(A.last())
                    xi = X[:, ds(c * CB + 2 * i, 2), :]
                    V.mark(nc.vector.tensor_tensor(xi, xi, fo[:, 2 * i:2 * i + 2, :], ALU.add))

            for e in (A, G):
                e.wait(Lv.last())
            o_normed = norm_o(0, scaled)
            M.wait(turn_context(0))
            put = project_T(kT, "k", bk_c, cT, 2)
            M.wait(put())
            values_put = put_values(project_values())
            M.wait(o_normed, values_put)
            project_o()
            join()
            cross(0, route=False)
            with Loop(nc, NC - 2, lines, "cross") as c:
                join()
                cross(c + 1)
            join()
            cross(NC - 1, more=False)
            join()

        for e in compute + [Lw]:
            e.wait(Lz.last())
        p2.close()
        with ExitStack() as s4:
            slot_i = sb("slot_i", [P, 2, NB], I32, s4)
            gate = sb("gate", [P, 2, NB], F32, s4)
            expert_of = sb("expert_of", [1, NT], I32, s4)
            W12 = sb("W12", [P, NE, KT, 2 * RH], F32, s4)
            W3 = sb("W3", [P, NE, KT, D], F32, s4)
            shared_there = Lx.last()
            hTs = sb("hTs", [P, SH // P, CT], F32, s4)
            sil = sb("sil", [P, 2, CT], F32, s4)
            xTs = (xT, norm.xn[:, :, :].rearrange("p b d -> p (b d)").rearrange("p (k t) -> p k t", k=KT))
            xT_there, f_done = {}, {}

            def fetch_xT(c):
                if c >= 2:
                    Lc.wait(f_done[c - 2], Lc.last())
                xTl = Lxt[c]
                xT_there[c] = xTl.mark(nc.sync.dma_start(xTs[c % 2][:, :, :], xT_all[c]))

            def shared(c):
                had = {}
                M.wait(xT_there[c])
                for f in range(SH // P):
                    if f >= 2:
                        M.wait(had[f - 2])
                    for w, bank in ((W1s, 2 * (f % 2)), (W2s, 2 * (f % 2) + 1)):
                        for k in range(KT):
                            r = nc.tensor.matmul(ps[:, bank, :], w[:, k, f * P:(f + 1) * P], xTs[c % 2][:, k, :],
                                                 start=(k == 0), stop=(k == KT - 1))
                    f_done[c] = M.mark(r)
                    A.wait(f_done[c])
                    V.wait(A.mark(nc.scalar.activation(sil[:, f % 2, :], ps[:, 2 * (f % 2), :], ACT.Silu)))
                    had[f] = V.mark(nc.vector.tensor_tensor(hTs[:, f, :], sil[:, f % 2, :], ps[:, 2 * (f % 2) + 1, :],
                                                            ALU.mult))
                    yield f
                M.wait(had[SH // P - 1])
                for j in range(CB):
                    for f in range(SH // P):
                        r = nc.tensor.matmul(ps[:, 4 + j, 0:D], hTs[:, f, j * P:(j + 1) * P], W3s[:, f, :],
                                             start=(f == 0), stop=(f == SH // P - 1))
                    V.wait(M.mark(r), V.last())
                    xj = X[:, c * CB + j, :]
                    V.mark(nc.vector.tensor_tensor(xj, ps[:, 4 + j, 0:D], xj, ALU.add))
                    yield SH // P + j

            fetch_xT(0)
            fetch_xT(1)
            for e in compute:
                e.wait(shared_there)
            chunk0 = shared(0)
            next(chunk0)
            norm3.stats(NC - 1)
            norm3.normalize(NC - 1)
            next(chunk0)
            last_turned = norm3.turn()
            route_store(NC - 1, last_turned)
            for e in range(0, NE, EL):
                for i, w in enumerate((rw1, rw2)):
                    Lr.mark(nc.sync.dma_start(
                        W12[:, e:e + EL, :, i * RH:(i + 1) * RH].rearrange("p e k f -> p (e k) f"),
                        w[e:e + EL].rearrange("e (k p) f -> p (e k) f", p=P)))
                Lr.mark(nc.sync.dma_start(W3[:, e:e + EL, :, :].rearrange("p e k d -> p (e k) d"),
                                          rw3[e:e + EL].rearrange("e (k p) d -> p (e k) d", p=P)))
            next(chunk0)
            M.wait(last_turned)
            route_logits(NC - 1, 5)
            A.wait(V.last())
            scored_all = A.mark(nc.scalar.activation(score[:, :, :], score[:, :, :], ACT.Sigmoid))
            XN_there = Lc.last()

            with ExitStack() as sr:
                sel = sb("sel", [P, NB, NE], F32, sr)
                eq = sb("eq", [P, NB, NE], F32, sr)
                top = sb("top", [P, NB], F32, sr)
                first = sb("first", [P, NB, NE], F32, sr)
                second = sb("second", [P, NB, NE], F32, sr)
                both = sb("both", [P, NB, NE], F32, sr)
                before = sb("before", [P, NB + 1, NE], F32, sr)
                back = sb("back", [P, NE], F32, sr)
                ones = sb("ones", [P, P], F32, sr)
                earlier = sb("earlier", [P, P], F32, sr)
                e_less = sb("e_less", [P, NE, NE], F32, sr)
                tile_no = sb("tile_no", [P, NT], F32, sr)
                tiles = sb("tiles", [P, NE], F32, sr)
                tiles_i = sb("tiles_i", [P, NE], I32, sr)
                first_tile = sb("first_tile", [P, NE], F32, sr)
                end_tile = sb("end_tile", [P, NE], F32, sr)
                ended = sb("ended", [P, NT, NE], F32, sr)
                slot = sb("slot", [P, NB, NE], F32, sr)
                G.mark(nc.gpsimd.iota(back[:, :], pattern=[[-1, NE]], base=NE, channel_multiplier=0,
                                      allow_small_or_imprecise_dtypes=True))
                G.mark(nc.gpsimd.iota(e_less[:, :, :], pattern=[[1, NE], [-1, NE]], base=0, channel_multiplier=0,
                                      allow_small_or_imprecise_dtypes=True))
                G.mark(nc.gpsimd.iota(tile_no[:, :], pattern=[[1, NT]], base=0, channel_multiplier=0,
                                      allow_small_or_imprecise_dtypes=True))
                G.mark(nc.gpsimd.memset(ones[:, :], 1.0))
                G.mark(nc.gpsimd.memset(earlier[:, :], 1.0))
                G.settle()
                G.mark(nc.gpsimd.affine_select(out=earlier[:, :], in_=earlier[:, :], compare_op=ALU.is_gt, fill=0.0,
                                               base=0, pattern=[[1, P]], channel_multiplier=-1))
                V.wait(G.last())

                turn_of = [0]

                def vec(ins):
                    V.mark(ins)
                    V.settle()
                    turn_of[0] += 1
                    if turn_of[0] % 8 == 0:
                        next(chunk0, None)

                def wide(v):
                    return v[:, :].unsqueeze(1).to_broadcast([P, NB, NE])

                def per_token(v):
                    return v.unsqueeze(2).to_broadcast([P, NB, NE])

                def flat(v):
                    return v[:, :, :].rearrange("p j e -> p (j e)")
                V.wait(scored_all)
                vec(nc.vector.tensor_tensor(sel[:, :, :], score[:, :, :], wide(eb), ALU.add))
                for chosen in (first, second):
                    vec(nc.vector.tensor_reduce(top[:, :], sel[:, :, :], AX_X, ALU.max))
                    vec(nc.vector.tensor_tensor(eq[:, :, :], sel[:, :, :], per_token(top[:, :]), ALU.is_equal))
                    vec(nc.vector.tensor_tensor(eq[:, :, :], eq[:, :, :], wide(back), ALU.mult))
                    vec(nc.vector.tensor_reduce(top[:, :], eq[:, :, :], AX_X, ALU.max))
                    vec(nc.vector.tensor_tensor(chosen[:, :, :], eq[:, :, :], per_token(top[:, :]), ALU.is_equal))
                    if chosen is first:
                        vec(nc.vector.scalar_tensor_tensor(flat(sel), flat(chosen), -3.0e38, flat(sel), ALU.mult, ALU.add))
                vec(nc.vector.tensor_tensor(both[:, :, :], first[:, :, :], second[:, :, :], ALU.add))
                vec(nc.vector.memset(before[:, 0, :], 0.0))
                for b in range(NB):
                    vec(nc.vector.tensor_tensor(before[:, b + 1, :], before[:, b, :], both[:, b, :], ALU.add))
                M.wait(V.last())
                nc.tensor.matmul(ps[:, 6, 0:NB * NE], earlier[:, :], flat(both), start=True, stop=False)
                nc.tensor.matmul(ps[:, 6, 0:NB * NE], ones[:, :], before[:, 0:NB, :].rearrange("p b e -> p (b e)"),
                                 start=False, stop=True)
                V.wait(M.mark(nc.tensor.matmul(ps[:, 7, 0:NE], ones[:, :], before[:, NB, :], start=True, stop=True)))
                vec(nc.vector.tensor_scalar(tiles_i[:, :], ps[:, 7, 0:NE], float(P - 1), None, ALU.add))
                vec(nc.vector.tensor_scalar(tiles_i[:, :], tiles_i[:, :], 7, None, ALU.logical_shift_right))
                vec(nc.vector.tensor_copy(tiles[:, :], tiles_i[:, :]))
                vec(nc.vector.tensor_scalar(e_less[:, :, :], e_less[:, :, :], 0.0, None, ALU.is_gt))
                vec(nc.vector.tensor_tensor(e_less[:, :, :], e_less[:, :, :],
                                            tiles[:, :].unsqueeze(1).to_broadcast([P, NE, NE]), ALU.mult))
                vec(nc.vector.tensor_reduce(first_tile[:, :], e_less[:, :, :], AX_X, ALU.add))
                vec(nc.vector.tensor_tensor(end_tile[:, :], first_tile[:, :], tiles[:, :], ALU.add))
                vec(nc.vector.tensor_scalar(first_tile[:, :], first_tile[:, :], float(P), None, ALU.mult))
                vec(nc.vector.tensor_tensor(slot[:, :, :], ps[:, 6, 0:NB * NE].rearrange("p (b e) -> p b e", b=NB),
                                            wide(first_tile), ALU.add))
                for i, chosen in enumerate((first, second)):
                    vec(nc.vector.tensor_tensor(eq[:, :, :], slot[:, :, :], chosen[:, :, :], ALU.mult))
                    vec(nc.vector.tensor_reduce(top[:, :], eq[:, :, :], AX_X, ALU.add))
                    vec(nc.vector.tensor_copy(slot_i[:, i, :], top[:, :]))
                G.wait(V.last())
                G.wait(Lz.last(), XN_there)
                for i in range(2):
                    for b in range(NB):
                        Ls.mark(nc.gpsimd.indirect_dma_start(
                            out=x_slots, out_offset=bass.IndirectOffsetOnAxis(ap=slot_i[:, i, b:b + 1].bitcast(U32), axis=0),
                            in_=XN[:, b, :], in_offset=None))
                for i, chosen in enumerate((first, second)):
                    vec(nc.vector.tensor_tensor(eq[:, :, :], score[:, :, :], chosen[:, :, :], ALU.mult))
                    vec(nc.vector.tensor_reduce(gate[:, i, :], eq[:, :, :], AX_X, ALU.add))
                vec(nc.vector.tensor_tensor(ended[0:1, :, :], end_tile[0:1, :].unsqueeze(1).to_broadcast([1, NT, NE]),
                                            tile_no[0:1, :].unsqueeze(2).to_broadcast([1, NT, NE]), ALU.is_le))
                vec(nc.vector.tensor_reduce(tile_no[0:1, :], ended[0:1, :, :], AX_X, ALU.add))
                vec(nc.vector.tensor_scalar(expert_of[0:1, :], tile_no[0:1, :], float(NE - 1), None, ALU.min))
                for _ in chunk0:
                    pass
            for _ in shared(1):
                pass
            fetch_xT(2)
            fetch_xT(3)
            join()
            for e in (nc.tensor,):
                e.wait_ge(Lr.sem, Lr.k)

            tiles_s = ExitStack()
            xg = sb("xg", [P, 2, D], F32, tiles_s)
            xt = sb("xt", [P, 2, KT, P], F32, tiles_s)
            sa = sb("sa", [P, 2, RH], F32, tiles_s)
            ht = sb("ht", [P, 2, KT, P], F32, tiles_s)
            yo = sb("yo", [P, 2, D], F32, tiles_s)
            for e in (nc.sync, nc.tensor):
                e.wait_ge(Ls.sem, Ls.k)

            def turn_x(n, p):
                Lc.wait(turned.at(n - 2))
                fetched[p].up(nc.sync.dma_start(xg[:, p, :], x_slots[ds(n * P, P), :]))
                M.wait(fetched[p].at((n - p) // 2), xcopied.at(n - 2))
                for k in range(KT):
                    r = nc.tensor.transpose(ps[:, p, k * P:(k + 1) * P], xg[:, p, k * P:(k + 1) * P], ident[:, :])
                turned.up(r)
                A.wait(turned.at(n), raised.at(n - 2))
                xcopied.up(nc.scalar.activation(xt[:, p, :, :].rearrange("p k t -> p (k t)"), ps[:, p, 0:D], ACT.Copy))

            def raise_(n, p):
                e = nc.tensor.value_load(expert_of[0:1, ds(n, 1)], min_val=0, max_val=NE - 1)
                M.wait(xcopied.at(n), gated.at(n - 2))
                for k in range(KT):
                    r = nc.tensor.matmul(ps[:, 2 + p, :], xt[:, p, k, :],
                                         W12[:, ds(e, 1), k, :].rearrange("p o f -> p (o f)"),
                                         start=(k == 0), stop=(k == KT - 1))
                raised.up(r)
                A.wait(raised.at(n), flipped.at(n - 2))
                acted.up(nc.scalar.activation(sa[:, p, :], ps[:, 2 + p, 0:RH], ACT.Silu))
                V.wait(acted.at(n))
                gated.up(nc.vector.tensor_tensor(sa[:, p, :], sa[:, p, :], ps[:, 2 + p, RH:2 * RH], ALU.mult))

            def flip(n, p):
                M.wait(gated.at(n), hcopied.at(n - 2))
                for k in range(KT):
                    r = nc.tensor.transpose(ps[:, 4 + p, k * P:(k + 1) * P], sa[:, p, k * P:(k + 1) * P], ident[:, :])
                flipped.up(r)
                A.wait(flipped.at(n), lowered.at(n - 2))
                hcopied.up(nc.scalar.activation(ht[:, p, :, :].rearrange("p k t -> p (k t)"), ps[:, 4 + p, 0:D], ACT.Copy))

            def lower(n, p):
                e = nc.tensor.value_load(expert_of[0:1, ds(n, 1)], min_val=0, max_val=NE - 1)
                M.wait(hcopied.at(n), yput.at(n - 2))
                for k in range(KT):
                    r = nc.tensor.matmul(ps[:, 6 + p, 0:D], ht[:, p, k, :],
                                         W3[:, ds(e, 1), k, :].rearrange("p o f -> p (o f)"),
                                         start=(k == 0), stop=(k == KT - 1))
                lowered.up(r)
                V.wait(lowered.at(n), stored[p].at((n - p) // 2 - 1))
                yput.up(nc.vector.tensor_copy(yo[:, p, :], ps[:, 6 + p, 0:D]))
                A.wait(yput.at(n))
                stored[p].up(nc.scalar.dma_start(y_slots[ds(n * P, P), :], yo[:, p, :]))

            turn_x(0, 0)
            turn_x(1, 1)
            raise_(0, 0)
            turn_x(2, 0)
            raise_(1, 1)
            flip(0, 0)
            with nc.Fori(0, (NT - 4) // 2) as i:
                for j in range(2):
                    turn_x(i * 2 + (3 + j), (1 + j) % 2)
                    raise_(i * 2 + (2 + j), j)
                    flip(i * 2 + (1 + j), (1 + j) % 2)
                    lower(i * 2 + j, j)
            n = NT - 3
            turn_x(n + 2, (n + 2) % 2)
            for n in range(NT - 3, NT + 1):
                for part, m in ((raise_, n + 1), (flip, n), (lower, n - 1)):
                    if m < NT:
                        part(m, m % 2)

            tiles_s.close()
            yg = sb("yg", [P, NB, D], F32, s4)
            back_to = (XN, yg)
            G.wait(stored[0].at(NT // 2 - 1), stored[1].at(NT // 2 - 1), Ls.last())
            for b in range(NB):
                for i in range(2):
                    gathered[2 * b // NB].mark(nc.gpsimd.indirect_dma_start(
                        out=back_to[i][:, b, :], out_offset=None, in_=y_slots,
                        in_offset=bass.IndirectOffsetOnAxis(ap=slot_i[:, i, b:b + 1].bitcast(U32), axis=0)))

            def add_routed(c, j):
                b = c * CB + j
                for i in range(2):
                    V.settle()
                    V.mark(nc.vector.scalar_tensor_tensor(X[:, b, :], back_to[i][:, b, :], gate[:, i, b:b + 1], X[:, b, :],
                                                          ALU.mult, ALU.add))

            def put_out(c):
                Lc.wait(V.last())
                nc.sync.dma_start(out.rearrange("b p d -> p b d")[:, ds(c * CB, CB), :],
                                  X[:, ds(c * CB, CB), :]).then_inc(out_stored, 16)

            for n in shared(NC - 2):
                if n == SH // P:
                    V.wait(gathered[0].last())
                if n >= SH // P:
                    add_routed(0, n - SH // P)
            put_out(0)
            for n in shared(NC - 1):
                if n == CB:
                    put_out(1)
                    V.wait(gathered[1].last())
                if n < SH // P:
                    add_routed(1 + n // CB, n % CB)
                elif n + 1 < SH // P + CB:
                    add_routed(NC - 1, n - SH // P + 1)
                if n == SH // P - 1:
                    add_routed(NC - 1, 0)
                    put_out(2)
            put_out(NC - 1)
            nc.sync.wait_ge(out_stored, 16 * NC)
            join()
        wts.close()


PER = {
    "qkv": [20, 10, 10, 6, 0, 96, 0],
    "cross": [48, 21, 21, 8, 0, 32, 0],
}

_INS = ['x', 'ctx_1024', 'L0_attn_W_qkv', 'L0_attn_W_proj', 'L0_attn_b_proj', 'L0_attn_lambda_q1',
        'L0_attn_lambda_k1', 'L0_attn_lambda_q2', 'L0_attn_lambda_k2', 'L0_attn_subln_w', 'L0_xattn_Wq',
        'L0_xattn_bq', 'L0_xattn_Wk', 'L0_xattn_bk', 'L0_xattn_Wv', 'L0_xattn_bv', 'L0_xattn_Wf', 'L0_xattn_bf',
        'L0_ffn_router_w', 'L0_ffn_expert_bias', 'L0_ffn_shared_w1', 'L0_ffn_shared_w2', 'L0_ffn_shared_w3',
        'L0_ffn_routed_w1', 'L0_ffn_routed_w2', 'L0_ffn_routed_w3']


def scratch(nc):
    return [nc.dram_tensor("qk_parts", (NB // 2, 4, 3, HD, MU, 2 * P), BF16, kind="Internal").ap(),
            nc.dram_tensor("xT_all", (NC, P, KT, CT), F32, kind="Internal").ap(),
            nc.dram_tensor("x_slots", (NT * P, D), F32, kind="Internal").ap(),
            nc.dram_tensor("y_slots", (NT * P, D), F32, kind="Internal").ap()]


def kernel(**inputs):
    import concourse.bacc as _bacc
    from concourse.bass_utils import run_bass_kernel_spmd as _run

    nc = _bacc.Bacc("TRN2", target_bir_lowering=False, num_devices=1)
    arrays, args = {}, []
    for name in _INS:
        a = np.ascontiguousarray(inputs[name])
        arrays[f"in_{name}_dram"] = a
        args.append(nc.dram_tensor(f"in_{name}_dram", a.shape, F32, kind="ExternalInput").ap())
    args.append(nc.dram_tensor("out_0_dram", (NB, P, D), F32, kind="ExternalOutput").ap())
    args += scratch(nc)
    decoder_layer(nc, *args)
    r = _run(nc, [arrays], core_ids=[0])
    return r.results[0]["out_0_dram"]
```
